# Optimizing a Trainium2 kernel written in Bass

```python
import numpy as np
import jax
import jax.numpy as jnp

def _softmax(x, axis=-1):
    return jax.nn.softmax(x, axis=axis)

def _gelu(x):
    return jax.nn.gelu(x, approximate=True)

def _silu(x):
    return jax.nn.silu(x)

def _sigmoid(x):
    return jax.nn.sigmoid(x)

def _layernorm(x, axis=-1, eps=1e-05):
    m = jnp.mean(x, axis=axis, keepdims=True)
    v = jnp.var(x, axis=axis, keepdims=True)
    return (x - m) / jnp.sqrt(v + eps)

def _scatter_add(tgt, idx, src, axis=0):
    return tgt.at[idx].add(src)

def _segment_sum(src, seg, n):
    return jax.ops.segment_sum(src, seg, n)
kernel_name = 'mk_sandwich_d1_jaxref_r8_199340'

def setup_inputs(seed: int=0):
    np.random.seed(seed)
    _w = jnp.asarray

    def _L0_attn_setup():
        import jax, jax.numpy as jnp
        import numpy as np
        H = 16
        CHUNK = 64
        EPS = 1e-05

        def _forward(x, wq, wk, wv, wo, fq1_w, fq1_b, fq2_w, fq2_b, fk1_w, fk1_b, fk2_w, fk2_b, norm_w):
            B, L, D = x.shape
            dk = D // H

            def proj(w):
                return (x @ w.T).reshape(B, L, H, dk).transpose(0, 2, 1, 3)
            q, k, v = (proj(wq), proj(wk), proj(wv))
            q = (q @ fq1_w.T + fq1_b) * (q @ fq2_w.T + fq2_b)
            k = (k @ fk1_w.T + fk1_b) * (k @ fk2_w.T + fk2_b)
            scale = dk ** (-0.5)
            n = L // CHUNK
            qc = q.reshape(B, H, n, CHUNK, dk) * scale
            kc = k.reshape(B, H, n, CHUNK, dk)
            vc = v.reshape(B, H, n, CHUNK, dk)
            kv = jnp.einsum('bhncd,bhnce->bhnde', kc, vc)
            kv = jnp.cumsum(kv, axis=2)
            kv = jnp.concatenate([jnp.zeros_like(kv[:, :, :1]), kv[:, :, :-1]], axis=2)
            inter = jnp.einsum('bhncd,bhnde->bhnce', qc, kv)
            s = jnp.einsum('bhncd,bhnmd->bhncm', qc, kc)
            mask = jnp.tril(jnp.ones((CHUNK, CHUNK), bool))
            s = jnp.where(mask, s, 0.0)
            intra = jnp.einsum('bhncm,bhnmd->bhncd', s, vc)
            o = (inter + intra).reshape(B, H, L, dk)
            o = o * jax.lax.rsqrt(jnp.mean(o * o, axis=-1, keepdims=True) + EPS) * norm_w
            o = o.transpose(0, 2, 1, 3).reshape(B, L, D)
            return o @ wo.T
        key = jax.random.key(seed)
        ks = jax.random.split(key, 16)
        B, L, D = (2, 512, 256)
        dk = D // H
        g = 2 ** (-2.5)

        def xav(k, n):
            lim = g * np.sqrt(6.0 / (2 * n))
            return jax.random.uniform(k, (n, n), jnp.float32, -lim, lim)
        return {'x': jax.random.normal(ks[0], (B, L, D), jnp.float32), 'wq': xav(ks[1], D), 'wk': xav(ks[2], D), 'wv': xav(ks[3], D), 'wo': xav(ks[4], D), 'fq1_w': xav(ks[5], dk), 'fq1_b': jnp.zeros((dk,), jnp.float32), 'fq2_w': xav(ks[6], dk), 'fq2_b': jnp.zeros((dk,), jnp.float32), 'fk1_w': xav(ks[7], dk), 'fk1_b': jnp.zeros((dk,), jnp.float32), 'fk2_w': xav(ks[8], dk), 'fk2_b': jnp.zeros((dk,), jnp.float32), 'norm_w': jnp.ones((dk,), jnp.float32)}
    _L0_attn_in = _L0_attn_setup()

    def _L0_ffn_setup():
        import jax, jax.numpy as jnp
        import numpy as np
        B, S, H = (1, 128, 256)
        NH, NKV, D = (32, 8, 64)
        GROUPS = NH // NKV
        E, F, TOPK = (8, 1024, 2)
        EPS = 1e-05

        def rmsnorm(x, w):
            return x * jax.lax.rsqrt(jnp.mean(x * x, axis=-1, keepdims=True) + EPS) * w

        def attention(h, wq, wk, wv, wo):
            b, s, _ = h.shape
            q = (h @ wq).reshape(b, s, NH, D).transpose(0, 2, 1, 3)
            k = (h @ wk).reshape(b, s, NKV, D).transpose(0, 2, 1, 3)
            v = (h @ wv).reshape(b, s, NKV, D).transpose(0, 2, 1, 3)
            k = jnp.repeat(k, GROUPS, axis=1)
            v = jnp.repeat(v, GROUPS, axis=1)
            scores = jnp.einsum('bhqd,bhkd->bhqk', q, k) / jnp.sqrt(jnp.float32(D))
            causal = jnp.tril(jnp.ones((s, s), bool))
            scores = jnp.where(causal, scores, jnp.finfo(scores.dtype).min)
            attn = jax.nn.softmax(scores, axis=-1)
            out = jnp.einsum('bhqk,bhkd->bhqd', attn, v)
            out = out.transpose(0, 2, 1, 3).reshape(b, s, NH * D)
            return out @ wo

        def moe(h, gate_w, w1, w2, w3):
            b, s, hd = h.shape
            t = h.reshape(-1, hd)
            T = t.shape[0]
            probs = jax.nn.softmax(t @ gate_w, axis=-1)
            topw, topi = jax.lax.top_k(probs, TOPK)
            topw = topw / jnp.sum(topw, axis=-1, keepdims=True)
            combine = jnp.zeros((T, E), t.dtype).at[jnp.arange(T)[:, None], topi].add(topw)
            up = jnp.einsum('th,ehf->etf', t, w1)
            gated = jax.nn.relu(up) * jnp.einsum('th,ehf->etf', t, w3)
            down = jnp.einsum('etf,efh->eth', gated, w2)
            out = jnp.einsum('eth,te->th', down, combine)
            return out.reshape(b, s, hd)
        key = jax.random.key(seed)
        ks = jax.random.split(key, 12)
        sc = 0.02
        return {'x': jax.random.normal(ks[0], (B, S, H), dtype=jnp.float32), 'ln1_w': jnp.ones((H,), jnp.float32), 'wq': jax.random.normal(ks[1], (H, NH * D), jnp.float32) * sc, 'wk': jax.random.normal(ks[2], (H, NKV * D), jnp.float32) * sc, 'wv': jax.random.normal(ks[3], (H, NKV * D), jnp.float32) * sc, 'wo': jax.random.normal(ks[4], (NH * D, H), jnp.float32) * sc, 'ln2_w': jnp.ones((H,), jnp.float32), 'gate_w': jax.random.normal(ks[5], (H, E), jnp.float32) * sc, 'w1': jax.random.normal(ks[6], (E, H, F), jnp.float32) * sc, 'w2': jax.random.normal(ks[7], (E, F, H), jnp.float32) * sc, 'w3': jax.random.normal(ks[8], (E, H, F), jnp.float32) * sc}
    _L0_ffn_in = _L0_ffn_setup()
    _d = {'L0_attn_x': _L0_attn_in['x'], 'L0_attn_wq': _L0_attn_in['wq'], 'L0_attn_wk': _L0_attn_in['wk'], 'L0_attn_wv': _L0_attn_in['wv'], 'L0_attn_wo': _L0_attn_in['wo'], 'L0_attn_fq1_w': _L0_attn_in['fq1_w'], 'L0_attn_fq1_b': _L0_attn_in['fq1_b'], 'L0_attn_fq2_w': _L0_attn_in['fq2_w'], 'L0_attn_fq2_b': _L0_attn_in['fq2_b'], 'L0_attn_fk1_w': _L0_attn_in['fk1_w'], 'L0_attn_fk1_b': _L0_attn_in['fk1_b'], 'L0_attn_fk2_w': _L0_attn_in['fk2_w'], 'L0_attn_fk2_b': _L0_attn_in['fk2_b'], 'L0_attn_norm_w': _L0_attn_in['norm_w'], 'L0_ffn_ln1_w': _L0_ffn_in['ln1_w'], 'L0_ffn_wq': _L0_ffn_in['wq'], 'L0_ffn_wk': _L0_ffn_in['wk'], 'L0_ffn_wv': _L0_ffn_in['wv'], 'L0_ffn_wo': _L0_ffn_in['wo'], 'L0_ffn_ln2_w': _L0_ffn_in['ln2_w'], 'L0_ffn_gate_w': _L0_ffn_in['gate_w'], 'L0_ffn_w1': _L0_ffn_in['w1'], 'L0_ffn_w2': _L0_ffn_in['w2'], 'L0_ffn_w3': _L0_ffn_in['w3']}
    _x0 = _d['L0_attn_x']
    _d['L0_attn_x'] = jax.random.normal(jax.random.fold_in(jax.random.key(seed), 1), (2, 1024, 256), dtype=_x0.dtype)
    del _x0
    return _d

def reference(L0_attn_x, L0_attn_wq, L0_attn_wk, L0_attn_wv, L0_attn_wo, L0_attn_fq1_w, L0_attn_fq1_b, L0_attn_fq2_w, L0_attn_fq2_b, L0_attn_fk1_w, L0_attn_fk1_b, L0_attn_fk2_w, L0_attn_fk2_b, L0_attn_norm_w, L0_ffn_ln1_w, L0_ffn_wq, L0_ffn_wk, L0_ffn_wv, L0_ffn_wo, L0_ffn_ln2_w, L0_ffn_gate_w, L0_ffn_w1, L0_ffn_w2, L0_ffn_w3):

    def _L0_attn_ref(x, wq, wk, wv, wo, fq1_w, fq1_b, fq2_w, fq2_b, fk1_w, fk1_b, fk2_w, fk2_b, norm_w):
        import jax, jax.numpy as jnp
        import numpy as np
        H = 16
        CHUNK = 64
        EPS = 1e-05

        def _forward(x, wq, wk, wv, wo, fq1_w, fq1_b, fq2_w, fq2_b, fk1_w, fk1_b, fk2_w, fk2_b, norm_w):
            B, L, D = x.shape
            dk = D // H

            def proj(w):
                return (x @ w.T).reshape(B, L, H, dk).transpose(0, 2, 1, 3)
            q, k, v = (proj(wq), proj(wk), proj(wv))
            q = (q @ fq1_w.T + fq1_b) * (q @ fq2_w.T + fq2_b)
            k = (k @ fk1_w.T + fk1_b) * (k @ fk2_w.T + fk2_b)
            scale = dk ** (-0.5)
            n = L // CHUNK
            qc = q.reshape(B, H, n, CHUNK, dk) * scale
            kc = k.reshape(B, H, n, CHUNK, dk)
            vc = v.reshape(B, H, n, CHUNK, dk)
            kv = jnp.einsum('bhncd,bhnce->bhnde', kc, vc)
            kv = jnp.cumsum(kv, axis=2)
            kv = jnp.concatenate([jnp.zeros_like(kv[:, :, :1]), kv[:, :, :-1]], axis=2)
            inter = jnp.einsum('bhncd,bhnde->bhnce', qc, kv)
            s = jnp.einsum('bhncd,bhnmd->bhncm', qc, kc)
            mask = jnp.tril(jnp.ones((CHUNK, CHUNK), bool))
            s = jnp.where(mask, s, 0.0)
            intra = jnp.einsum('bhncm,bhnmd->bhncd', s, vc)
            o = (inter + intra).reshape(B, H, L, dk)
            o = o * jax.lax.rsqrt(jnp.mean(o * o, axis=-1, keepdims=True) + EPS) * norm_w
            o = o.transpose(0, 2, 1, 3).reshape(B, L, D)
            return o @ wo.T
        return _forward(x, wq, wk, wv, wo, fq1_w, fq1_b, fq2_w, fq2_b, fk1_w, fk1_b, fk2_w, fk2_b, norm_w)

    def _L0_ffn_ref(x, ln1_w, wq, wk, wv, wo, ln2_w, gate_w, w1, w2, w3):
        import jax, jax.numpy as jnp
        import numpy as np
        B, S, H = (1, 128, 256)
        NH, NKV, D = (32, 8, 64)
        GROUPS = NH // NKV
        E, F, TOPK = (8, 1024, 2)
        EPS = 1e-05

        def rmsnorm(x, w):
            return x * jax.lax.rsqrt(jnp.mean(x * x, axis=-1, keepdims=True) + EPS) * w

        def attention(h, wq, wk, wv, wo):
            b, s, _ = h.shape
            q = (h @ wq).reshape(b, s, NH, D).transpose(0, 2, 1, 3)
            k = (h @ wk).reshape(b, s, NKV, D).transpose(0, 2, 1, 3)
            v = (h @ wv).reshape(b, s, NKV, D).transpose(0, 2, 1, 3)
            k = jnp.repeat(k, GROUPS, axis=1)
            v = jnp.repeat(v, GROUPS, axis=1)
            scores = jnp.einsum('bhqd,bhkd->bhqk', q, k) / jnp.sqrt(jnp.float32(D))
            causal = jnp.tril(jnp.ones((s, s), bool))
            scores = jnp.where(causal, scores, jnp.finfo(scores.dtype).min)
            attn = jax.nn.softmax(scores, axis=-1)
            out = jnp.einsum('bhqk,bhkd->bhqd', attn, v)
            out = out.transpose(0, 2, 1, 3).reshape(b, s, NH * D)
            return out @ wo

        def moe(h, gate_w, w1, w2, w3):
            b, s, hd = h.shape
            t = h.reshape(-1, hd)
            T = t.shape[0]
            probs = jax.nn.softmax(t @ gate_w, axis=-1)
            topw, topi = jax.lax.top_k(probs, TOPK)
            topw = topw / jnp.sum(topw, axis=-1, keepdims=True)
            combine = jnp.zeros((T, E), t.dtype).at[jnp.arange(T)[:, None], topi].add(topw)
            up = jnp.einsum('th,ehf->etf', t, w1)
            gated = jax.nn.relu(up) * jnp.einsum('th,ehf->etf', t, w3)
            down = jnp.einsum('etf,efh->eth', gated, w2)
            out = jnp.einsum('eth,te->th', down, combine)
            return out.reshape(b, s, hd)
        h = x + attention(rmsnorm(x, ln1_w), wq, wk, wv, wo)
        return h + moe(rmsnorm(h, ln2_w), gate_w, w1, w2, w3)
    x = L0_attn_x
    x = x + _layernorm(_L0_attn_ref(_layernorm(x, axis=-1), L0_attn_wq, L0_attn_wk, L0_attn_wv, L0_attn_wo, L0_attn_fq1_w, L0_attn_fq1_b, L0_attn_fq2_w, L0_attn_fq2_b, L0_attn_fk1_w, L0_attn_fk1_b, L0_attn_fk2_w, L0_attn_fk2_b, L0_attn_norm_w), axis=-1)
    x = x + _layernorm(_L0_ffn_ref(_layernorm(x, axis=-1), L0_ffn_ln1_w, L0_ffn_wq, L0_ffn_wk, L0_ffn_wv, L0_ffn_wo, L0_ffn_ln2_w, L0_ffn_gate_w, L0_ffn_w1, L0_ffn_w2, L0_ffn_w3), axis=-1)
    return x

_drawn_inputs = setup_inputs


def setup_inputs(seed=0):
    import zlib

    import numpy as np

    out = dict(_drawn_inputs(seed))
    spreads = {'L0_attn_fq1_b': (0.0, 0.1),
     'L0_attn_fq2_b': (0.0, 0.1),
     'L0_attn_fk1_b': (0.0, 0.1),
     'L0_attn_fk2_b': (0.0, 0.1),
     'L0_attn_norm_w': (1.0, 0.2),
     'L0_ffn_ln1_w': (1.0, 0.6),
     'L0_ffn_ln2_w': (1.0, 0.6)}
    factors = {'L0_ffn_wq': 8.0,
     'L0_ffn_wk': 8.0,
     'L0_ffn_gate_w': 4.102,
     'L0_ffn_w1': 4.45,
     'L0_ffn_w2': 3.707,
     'L0_ffn_w3': 3.686}
    for name, (base, spread) in spreads.items():
        noise = np.random.default_rng([zlib.crc32(name.encode()), seed]).standard_normal(out[name].shape)
        drawn = base * np.exp(spread * noise) if base else spread * noise
        out[name] = jnp.asarray(drawn.astype(out[name].dtype))
    for name, factor in factors.items():
        out[name] = (out[name] * factor).astype(out[name].dtype)
    return out
```

```python
from contextlib import ExitStack

import concourse.bass as bass
from concourse import mybir

F32 = mybir.dt.float32
F32R = mybir.dt.float32r
BF16 = mybir.dt.bfloat16
U32 = mybir.dt.uint32
ALU = mybir.AluOpType
ACT = mybir.ActivationFunctionType
AX = mybir.AxisListType

P = 128
D = 256
KB = D // P
BATCH, SEQ = 2, 1024
NT = BATCH * SEQ // P
TB = SEQ // P
H1, DK = 16, 16
HB = P // DK
NH, NKV, DH = 32, 8, 64
G = NH // NKV
E, F = 8, 1024
FB = F // P
TG = 512
NG = BATCH * SEQ // TG
HALF = SEQ // 2
EPS = 1e-5
MASKED = -1e30


def pairs_of(ct, h):
    return range((ct + 1) * h // G, (ct + 1) * (h + 1) // G)


def build(nc, a, out):
    ctx = ExitStack()
    with ctx:
        def sb(name, shape, dt=F32):
            return ctx.enter_context(nc.sbuf_tensor(name, shape, dt))

        def wait_alone(engine, sem, value):
            value = engine.to_reg(value)
            engine.wait_ge(S("constants_ready"), 12)
            engine.wait_ge(sem, value)

        sems = {}

        def S(name):
            if name not in sems:
                sems[name] = ctx.enter_context(nc.semaphore(name))
            return sems[name]

        bank = [ctx.enter_context(nc.psum_tensor(f"bank{i}", [P, 512], F32)) for i in range(4)]
        wide = ctx.enter_context(nc.psum_tensor("wide", [P, 4, 512], F32))

        x_all = sb("x_all", [P, NT, D])
        acc = sb("acc", [P, NT, D])
        rT_all = sb("rT_all", [P, KB, NT * P])
        wo2 = sb("wo2", [P, NKV, 2, D])
        comb = sb("comb", [P, NT, E])
        ident = sb("ident", [P, P])
        identb = sb("identb", [P, P], BF16)
        tri = sb("tri", [P, P])
        above = sb("above", [P, P], BF16)
        headmask = sb("headmask", [P, HB])
        experts = sb("experts", [P, E])
        neghalf = sb("neghalf", [P, H1])
        w1_e = [sb(f"w1_e{i}", [P, KB, F]) for i in range(2)]
        w3_e = [sb(f"w3_e{i}", [P, KB, F]) for i in range(2)]
        w2_e = [sb(f"w2_e{i}", [P, FB, D]) for i in range(2)]
        wnat = w2_e[1][:].rearrange("p (w k) d -> p w k d", w=4)
        fnat = sb("fnat", [P, 4, DK])
        fdiag = sb("fdiag", [P, 4, HB, DK])
        fdiagT = sb("fdiagT", [P, 4, P])
        wfeat = w1_e[0][:].rearrange("p k (w d) -> p w k d", w=4)
        wvT = w3_e[0][:, 0, 0:KB * D].rearrange("p (k d) -> p k d", k=KB)
        woT = w3_e[0][:, 1, 0:KB * D].rearrange("p (k d) -> p k d", k=KB)
        fbias = sb("fbias", [P, 4])
        fbias_q = sb("fbias_q", [P, 1])
        normw = sb("normw", [P, 1])
        ln1 = sb("ln1", [P, KB])
        ln2 = sb("ln2", [P, KB])
        gate = sb("gate", [P, KB, E])
        st6 = sb("st6", [P, 6])
        mv = sb("mv", [P, 2])
        ve = sb("ve", [P, 1])
        rstd = sb("rstd", [P, 1])
        xn = sb("xn", [P, D])
        xnT = sb("xnT", [P, KB, P])
        q1s = sb("q1s", [P, KB, P])
        k1s = sb("k1s", [P, KB, P])
        qT = sb("qT", [P, KB, P])
        kT = sb("kT", [P, KB, P])
        qx = w1_e[1][:].rearrange("p k (h c) -> p k h c", h=HB)
        ktok = sb("ktok", [P, D])
        vtok = sb("vtok", [P, D])
        sm = w3_e[1][:].rearrange("p k (h c) -> p (k h) c", c=P)
        kvt = sb("kvt", [P, KB, P])
        state = sb("state", [P, KB, P])
        osq = sb("osq", [P, D])
        oss = sb("oss", [P, H1])
        ove = sb("ove", [P, H1])
        orstd = sb("orstd", [P, H1])
        on = sb("on", [P, D])
        onT = sb("onT", [P, KB, P])
        wq_g = sb("wq_g", [P, KB, G * DH])
        wkv_g = sb("wkv_g", [P, KB, 2 * DH])
        qhl = sb("qhl", [P, G, SEQ], F32R)
        khi = sb("khi", [P, SEQ], F32R)
        klo = sb("klo", [P, SEQ], F32R)
        vT = sb("vT", [DH, SEQ])
        vt = sb("vt", [P, TB, DH])
        probs = sb("probs", [P, 2, G, SEQ])
        nmax = sb("nmax", [P, 2, G])
        rsum = sb("rsum", [P, 2, G])
        rinv = sb("rinv", [P, 2, G])
        pT = [sb(f"pT{i}", [P, G * P]) for i in range(2)]
        oT = sb("oT", [P, 2, P])
        relu = pT
        top = sb("top", [P, 8])
        topi = sb("topi", [P, 8], U32)
        topf = sb("topf", [P, 8])
        topw = sb("topw", [P, 2])
        pick = sb("pick", [P, 2, E])
        cw = sb("cw", [P, TG // P])
        gated = probs[:].rearrange("p a g s -> p (a g s)")[:, 0:FB * TG].rearrange("p (f t) -> p f t", f=FB)
        combe = sb("combe", [P, NT])

        block = ctx.enter_context(nc.Block())

        @block.sync
        def _(sp):
            sp.dma_start(x_all[:], a["L0_attn_x"].rearrange("b (t p) d -> p (b t) d", p=P)).then_inc(S("x_loaded"), 16)
            for n, w in enumerate(("wq", "wk", "wv", "wo")):
                sp.dma_start(wnat[:, n], a[f"L0_attn_{w}"].rearrange("(k p) d -> p k d", p=P)).then_inc(S("wnat_loaded"), 16)
            for n, w in enumerate(("fq1", "fq2", "fk1", "fk2")):
                for h in range(HB):
                    rows = slice(h * DK, (h + 1) * DK)
                    sp.dma_start(fnat[rows, n], a[f"L0_attn_{w}_w"]).then_inc(S("small_loaded"), 16)
                    sp.dma_start(fbias[rows, n:n + 1], a[f"L0_attn_{w}_b"].rearrange("(e o) -> e o", o=1)).then_inc(S("small_loaded"), 16)
            for h in range(HB):
                sp.dma_start(normw[h * DK:(h + 1) * DK], a["L0_attn_norm_w"].rearrange("(e o) -> e o", o=1)).then_inc(S("small_loaded"), 16)
            for t, w in ((ln1, "ln1_w"), (ln2, "ln2_w")):
                for k in range(KB):
                    sp.dma_start(t[:, k:k + 1], a[f"L0_ffn_{w}"][k * P:(k + 1) * P].rearrange("(e o) -> e o", o=1)).then_inc(S("small_loaded"), 16)
            sp.dma_start(gate[:], a["L0_ffn_gate_w"].rearrange("(k p) e -> p k e", p=P)).then_inc(S("small_loaded"), 16)
            wo_v = a["L0_ffn_wo"].rearrange("(g u j d) n -> u d g j n", g=NKV, u=2, j=2)
            for u in range(2):
                for g in range(NKV):
                    sp.dma_start(wo2[u * DH:(u + 1) * DH, g], wo_v[u][:, g]).then_inc(S("wo2_loaded"), 16)
            wq_v = a["L0_ffn_wq"].rearrange("(k p) n -> p k n", p=P)
            wk_v = a["L0_ffn_wk"].rearrange("(k p) n -> p k n", p=P)
            wv_v = a["L0_ffn_wv"].rearrange("(k p) n -> p k n", p=P)
            with sp.Fori(0, BATCH) as b:
                with sp.Fori(0, NKV) as g:
                    n = b * NKV + g
                    sp.wait_ge(S("projected"), n * 6)
                    sp.dma_start(wq_g[:], wq_v[:, :, bass.ds(g * (G * DH), G * DH)]).then_inc(S("wq_loaded"), 16)
                    sp.dma_start(wkv_g[:, :, 0:DH], wk_v[:, :, bass.ds(g * DH, DH)]).then_inc(S("wk_loaded"), 16)
                    sp.dma_start(wkv_g[:, :, DH:2 * DH], wv_v[:, :, bass.ds(g * DH, DH)]).then_inc(S("wv_loaded"), 16)
            w1_v = a["L0_ffn_w1"].rearrange("e (k p) f -> p e k f", p=P)
            w3_v = a["L0_ffn_w3"].rearrange("e (k p) f -> p e k f", p=P)
            w2_v = a["L0_ffn_w2"].rearrange("e (f p) d -> p e f d", p=P)

            def load_expert(e, s):
                sp.dma_start(w1_e[s][:], w1_v[:, bass.ds(e, 1)].rearrange("p o k f -> p (o k) f")).then_inc(S(f"w1_loaded{s}"), 16)
                sp.dma_start(w3_e[s][:], w3_v[:, bass.ds(e, 1)].rearrange("p o k f -> p (o k) f")).then_inc(S(f"w3_loaded{s}"), 16)
                sp.dma_start(w2_e[s][:], w2_v[:, bass.ds(e, 1)].rearrange("p o f d -> p (o f) d")).then_inc(S(f"w2_loaded{s}"), 16)

            sp.wait_ge(S("rT_ready"), NT)
            for s in range(2):
                load_expert(s, s)
            with sp.Fori(1, E // 2) as e2:
                for s in range(2):
                    sp.wait_ge(S("down_psum"), (e2 * 2 + (s - 1)) * NG)
                    load_expert(e2 * 2 + s, s)
            out_v = out.rearrange("b (t p) d -> p (b t) d", p=P)
            with sp.Fori(0, NT) as i:
                sp.wait_ge(S("out_ready"), i + 1)
                sp.dma_start(out_v[:, bass.ds(i, 1)], x_all[:, bass.ds(i, 1)]).then_inc(S("stored"), 16)
            sp.wait_ge(S("stored"), 16 * NT)

        @block.gpsimd
        def _(gp):
            nc.gpsimd.memset(ident[:], 0.0).then_inc(S("constants_ready"), 1)
            nc.gpsimd.memset(tri[:], 1.0).then_inc(S("constants_ready"), 1)
            nc.gpsimd.memset(above[:], 0.0).then_inc(S("constants_ready"), 1)
            nc.gpsimd.memset(headmask[:], 1.0).then_inc(S("constants_ready"), 1)
            nc.gpsimd.memset(neghalf[:], -0.5).then_inc(S("constants_ready"), 1)
            nc.gpsimd.iota(experts[:], [[1, E]], base=0, channel_multiplier=0,
                           allow_small_or_imprecise_dtypes=True).then_inc(S("constants_ready"), 1)
            gp.wait_ge(S("constants_ready"), 6)
            nc.gpsimd.affine_select(out=ident[:], in_=ident[:], compare_op=ALU.not_equal, fill=1.0, base=0,
                                    pattern=[[-1, P]], channel_multiplier=1).then_inc(S("constants_ready"), 1)
            nc.gpsimd.affine_select(out=tri[:], in_=tri[:], compare_op=ALU.is_ge, fill=0.0, base=0,
                                    pattern=[[1, P]], channel_multiplier=-1).then_inc(S("constants_ready"), 1)
            nc.gpsimd.affine_select(out=above[:], in_=above[:], compare_op=ALU.is_ge, fill=MASKED, base=0,
                                    pattern=[[-1, P]], channel_multiplier=1).then_inc(S("constants_ready"), 1)
            nc.gpsimd.affine_select(out=headmask[:], in_=headmask[:], compare_op=ALU.is_ge, fill=0.0, base=0,
                                    pattern=[[-DK, HB]], channel_multiplier=1).then_inc(S("constants_ready"), 1)
            gp.wait_ge(S("constants_ready"), 10)
            nc.gpsimd.affine_select(out=headmask[:], in_=headmask[:], compare_op=ALU.is_ge, fill=0.0, base=DK - 1,
                                    pattern=[[DK, HB]], channel_multiplier=-1).then_inc(S("constants_ready"), 1)
            nc.gpsimd.tensor_copy(identb[:], ident[:]).then_inc(S("constants_ready"), 1)
            gp.wait_ge(S("constants_ready"), 12)
            gp.wait_ge(S("small_loaded"), 16 * (16 * 4 + HB + 2 * KB + 1))
            for n in range(4):
                ins = nc.gpsimd.tensor_tensor(fdiag[:, n], fnat[:, n:n + 1, :].to_broadcast([P, HB, DK]),
                                              headmask[:].rearrange("p (h o) -> p h o", o=1).to_broadcast([P, HB, DK]), ALU.mult)
            ins.then_inc(S("fdiag_ready"), 1)

            def power(i, n, dst, src, asked, given):
                gp.wait_ge(S(asked), i + 1)
                nc.gpsimd.tensor_tensor(dst, src, neghalf[:, 0:n], ALU.pow).then_inc(S(given), 1)

            with gp.Fori(0, NT) as i:
                power(i, 1, rstd[:], ve[:], "ve_x", "rstd_x")
                gp.wait_ge(S("qT_ready"), i + 1)
                gp.wait_ge(S("scores1"), i)
                for k in range(KB):
                    ins = nc.gpsimd.tensor_tensor(
                        qx[:, k], qT[:, k:k + 1, :].to_broadcast([P, HB, P]),
                        headmask[:].rearrange("p (h o) -> p h o", o=1).to_broadcast([P, HB, P]), ALU.mult)
                ins.then_inc(S("qx_ready"), 1)
                power(i, H1, orstd[:], ove[:], "ve_o", "rstd_o")
                power(i, 1, rstd[:], ve[:], "ve_ao", "rstd_ao")
                power(i, 1, rstd[:], ve[:], "ve_x1", "rstd_x1")
                power(i, 1, rstd[:], ve[:], "ve_y", "rstd_y")
            with gp.Fori(0, BATCH * NKV) as n:
                for ct in range(TB):
                    for h in range(G):
                        c = ct * G + h
                        wait_alone(gp, S("rinv_ready"), n * (TB * G) + c + 1)
                        w = (ct + 1) * P
                        nc.gpsimd.tensor_scalar(probs[:, ct % 2, h, 0:w], probs[:, ct % 2, h, 0:w],
                                                rinv[:, ct % 2, h:h + 1], None, ALU.mult).then_inc(S("probs_ready"), 1)
            with gp.Fori(0, NT) as i:
                power(i, 1, rstd[:], ve[:], "ve_h", "rstd_h")
            with gp.Fori(0, NT) as i:
                power(i, 1, rstd[:], ve[:], "ve_f", "rstd_f")

        @block.scalar
        def _(act):
            for n in range(4):
                act.wait_ge(S("fT_psum"), n + 1)
                nc.scalar.copy(fdiagT[:, n], bank[0][:, 0:P]).then_inc(S("fT_ready"), 1)
            for n in range(4):
                for k in range(KB):
                    act.wait_ge(S("wfeat_psum"), n * KB + k + 1)
                    nc.scalar.copy(wfeat[:, n, k], bank[0][:, 0:D]).then_inc(S("wfeat_ready"), 1)
            for k in range(KB):
                act.wait_ge(S("wvT_psum"), k + 1)
                nc.scalar.copy(wvT[:, k], bank[0][:, 0:D]).then_inc(S("wvT_ready"), 1)
            for k in range(KB):
                act.wait_ge(S("woT_psum"), k + 1)
                nc.scalar.activation(woT[:, k], bank[0][:, 0:D], ACT.Copy, scale=normw[:, 0:1]).then_inc(S("woT_ready"), 1)
            nc.scalar.activation(fbias_q[:], fbias[:, 0:1], ACT.Copy, scale=DK ** -0.5).then_inc(S("fbias_q_ready"), 1)
            act.wait_ge(S("fbias_q_ready"), 1)
            with act.Fori(0, NT) as i:
                act.wait_ge(S("xnT_psum"), i + 1)
                act.wait_ge(S("v_psum"), i)
                nc.scalar.copy(xnT[:], bank[0][:, 0:D].rearrange("p (k c) -> p k c", k=KB)).then_inc(S("xnT_ready"), 1)
                act.wait_ge(S("q_psum"), i + 1)
                act.wait_ge(S("qT_ready"), i)
                nc.scalar.activation(q1s[:], bank[1][:, 0:D].rearrange("p (k c) -> p k c", k=KB), ACT.Identity, bias=fbias_q[:, 0:1],
                                     scale=DK ** -0.5).then_inc(S("q1_ready"), 1)
                act.wait_ge(S("k_psum"), i + 1)
                act.wait_ge(S("kT_ready"), i)
                nc.scalar.activation(k1s[:], bank[2][:, 0:D].rearrange("p (k c) -> p k c", k=KB), ACT.Identity, bias=fbias[:, 2:3]).then_inc(S("k1_ready"), 1)
                act.wait_ge(S("v_psum"), i + 1)
                act.wait_ge(S("o_psum"), i)
                act.wait_ge(S("kv_psum"), i)
                nc.scalar.copy(vtok[:], bank[3][:, 0:D]).then_inc(S("v_ready"), 1)
                act.wait_ge(S("ktok_psum"), i + 1)
                nc.scalar.copy(ktok[:], bank[0][:, 0:D]).then_inc(S("ktok_ready"), 1)
                act.wait_ge(S("o_psum"), i + 1)
                act.wait_ge(S("oss_ready"), i)
                act.wait_ge(S("yss_ready"), i)
                nc.scalar.activation(osq[:], bank[1][:, 0:D], ACT.Square).then_inc(S("osq_ready"), 1)
                act.wait_ge(S("onT_psum"), i + 1)
                nc.scalar.copy(onT[:], bank[0][:, 0:D].rearrange("p (k c) -> p k c", k=KB)).then_inc(S("onT_ready"), 1)
                act.wait_ge(S("y_ready"), i + 1)
                nc.scalar.activation(osq[:], acc[:, bass.ds(i, 1)], ACT.Square, accum_out=rsum[:, 0, 0:1]).then_inc(S("yss_ready"), 1)
                act.wait_ge(S("rT_psum"), i + 1)
                for k in range(KB):
                    ins = nc.scalar.activation(rT_all[:, k, bass.ds(i * P, P)], bank[0][:, k * P:(k + 1) * P], ACT.Copy,
                                               scale=ln1[:, k:k + 1])
                ins.then_inc(S("rT_ready"), 1)
            with act.Fori(0, BATCH * NKV) as n:
                for t in range(2):
                    cols = slice(t * HALF, (t + 1) * HALF)
                    act.wait_ge(S("projected"), n * 6 + t + 1)
                    for u in range(2):
                        ins = nc.scalar.copy(khi[u * DH:(u + 1) * DH, cols], wide[0:DH, t, :])
                    ins.then_inc(S("khi_ready"), 1)
                    nc.scalar.copy(vT[:, cols], wide[DH:P, t, :]).then_inc(S("vT_ready"), 1)
                for m in range(4):
                    act.wait_ge(S("projected"), n * 6 + 2 + m + 1)
                    for u in range(2):
                        ins = nc.scalar.activation(qhl[0:DH, 2 * (m // 2) + u, (m % 2) * HALF:(m % 2 + 1) * HALF],
                                                   wide[u * DH:(u + 1) * DH, (2 + m) % 4, :], ACT.Copy, scale=DH ** -0.5)
                    ins.then_inc(S("qhi_ready"), 1)

                def evac_pT(ct, m):
                    j = ct * (ct + 1) // 2 + m
                    if j % 2 == 0:
                        act.wait_ge(S("pT_psum"), n * 36 + j + 1)
                        nc.scalar.copy(pT[0][:], bank[0][:]).then_inc(S("pT_even"), 1)

                for ct in range(TB + 1):
                    for h in range(G):
                        if ct < TB:
                            c = ct * G + h
                            w = (ct + 1) * P
                            act.wait_ge(S("nmax_ready"), n * (TB * G) + c + 1)
                            nc.scalar.activation(probs[:, ct % 2, h, 0:w],
                                                 wide[:, 2 * (h % 2):2 * (h % 2) + 2, :].rearrange("p a b -> p (a b)")[:, 0:w],
                                                 ACT.Exp, bias=nmax[:, ct % 2, h:h + 1],
                                                 accum_out=rsum[:, ct % 2, h:h + 1]).then_inc(S("exp_done"), 1)
                        if ct > 0:
                            for m in pairs_of(ct - 1, h):
                                evac_pT(ct - 1, m)
                    if ct > 0:
                        act.wait_ge(S("o2_psum"), n * TB + ct)
                        nc.scalar.copy(oT[:], bank[2][:, 0:2 * P].rearrange("p (j c) -> p j c", j=2)).then_inc(S("oT_ready"), 1)
            with act.Fori(0, NT) as i:
                if True:
                    act.wait_ge(S("acc_done"), BATCH * NKV * TB)
                    act.wait_ge(S("ve_h"), i)
                    act.wait_ge(S("hss_ready"), i)
                    nc.scalar.activation(osq[:], acc[:, bass.ds(i, 1)], ACT.Square, accum_out=rsum[:, 0, 0:1]).then_inc(S("hss_ready"), 1)
                    act.wait_ge(S("tT_psum"), i + 1)
                    act.wait_ge(S("logits_psum"), i)
                    act.wait_ge(S("tT_copied"), i)
                    for k in range(KB):
                        ins = nc.scalar.activation(xnT[:, k], bank[0][:, k * P:(k + 1) * P], ACT.Copy, scale=ln2[:, k:k + 1])
                    ins.then_inc(S("tT_ready"), 1)
                    act.wait_ge(S("lmax_ready"), i + 1)
                    nc.scalar.activation(oss[:, 0:E], bank[1][:, 0:E], ACT.Exp, bias=nmax[:, 0, 0:1],
                                         accum_out=rsum[:, 0, 1:2]).then_inc(S("gexp_ready"), 1)
            with act.Fori(0, E // 2) as e2:
                for s in range(2):
                    with act.Fori(0, NG) as tg:
                        n = (e2 * 2 + s) * NG + tg
                        for f in range(FB):
                            act.wait_ge(S("up_psum"), n * FB + f + 1)
                            if f >= 2:
                                act.wait_ge(S("gated_ready"), n * FB + f - 1)
                            else:
                                act.wait_ge(S("gated_ready"), n * FB)
                            nc.scalar.activation(relu[f % 2][:], wide[:, f % 2, :], ACT.Relu).then_inc(S("relu_ready"), 1)

        @block.vector
        def _(v):
            def inv_std(i, src, asked, mean_in_mv=True):
                nc.vector.bn_stats(st6[:], src).then_inc(S(asked + "_st"), 1)
                wait_alone(v, S(asked + "_st"), i + 1)
                nc.vector.bn_aggr(mv[:], st6[:]).then_inc(S(asked + "_mv"), 1)
                v.wait_ge(S(asked + "_mv"), i + 1)
                nc.vector.tensor_scalar(ve[:], mv[:, 1:2], EPS, None, ALU.add).then_inc(S(asked), 1)

            v.wait_ge(S("x_loaded"), 16)
            with v.Fori(0, BATCH) as b:
                v.wait_ge(S("o_psum"), b * TB)
                v.wait_ge(S("state_ready"), b * TB)
                nc.vector.memset(state[:], 0.0).then_inc(S("state_clear"), 1)
                wait_alone(v, S("state_clear"), b + 1)
                with v.Fori(0, TB) as t:
                    i = b * TB + t
                    xt = x_all[:, bass.ds(i, 1)]
                    at = acc[:, bass.ds(i, 1)]
                    inv_std(i, xt, "ve_x")
                    v.wait_ge(S("rstd_x"), i + 1)
                    nc.vector.tensor_scalar(xn[:], xt, mv[:, 0:1], rstd[:], ALU.subtract, ALU.mult).then_inc(S("xn_ready"), 1)
                    v.wait_ge(S("q1_ready"), i + 1)
                    v.wait_ge(S("o_psum"), i)
                    nc.vector.scalar_tensor_tensor(out=qT[:], in0=bank[1][:, D:2 * D].rearrange("p (k c) -> p k c", k=KB), scalar=fbias[:, 1:2], in1=q1s[:],
                                                   op0=ALU.add, op1=ALU.mult).then_inc(S("qT_ready"), 1)
                    v.wait_ge(S("k1_ready"), i + 1)
                    nc.vector.scalar_tensor_tensor(out=kT[:], in0=bank[2][:, D:2 * D].rearrange("p (k c) -> p k c", k=KB), scalar=fbias[:, 3:4], in1=k1s[:],
                                                   op0=ALU.add, op1=ALU.mult).then_inc(S("kT_ready"), 1)
                    v.wait_ge(S("scores1"), i + 1)
                    nc.vector.tensor_tensor(sm[:], wide[:].rearrange("p a (h c) -> p (a h) c", c=P),
                                            tri[:].rearrange("p (o c) -> p o c", o=1).to_broadcast([P, H1, P]), ALU.mult).then_inc(S("sm_ready"), 1)
                    v.wait_ge(S("kv_psum"), i + 1)
                    v.wait_ge(S("state_ready"), i)
                    nc.vector.tensor_tensor(kvt[:].rearrange("p k (h e) -> p k h e", h=HB),
                                            bank[2][:, 0:D].rearrange("p (k h e) -> p k h e", k=KB, h=HB),
                                            headmask[:].rearrange("p (o h q) -> p o h q", o=1, q=1).to_broadcast([P, KB, HB, DK]),
                                            ALU.mult).then_inc(S("kvt_ready"), 1)
                    v.wait_ge(S("kvt_ready"), i + 1)
                    v.wait_ge(S("o_psum"), i + 1)
                    nc.vector.tensor_tensor(state[:], state[:], kvt[:], ALU.add).then_inc(S("state_ready"), 1)
                    v.wait_ge(S("osq_ready"), i + 1)
                    nc.vector.tensor_reduce(oss[:], osq[:].rearrange("p (h e) -> p h e", h=H1), AX.X, ALU.add).then_inc(S("oss_ready"), 1)
                    v.wait_ge(S("oss_ready"), i + 1)
                    nc.vector.tensor_scalar(ove[:], oss[:], 1.0 / DK, EPS, ALU.mult, ALU.add).then_inc(S("ve_o"), 1)
                    v.wait_ge(S("rstd_o"), i + 1)
                    nc.vector.tensor_tensor(on[:].rearrange("p (h e) -> p h e", h=H1), bank[1][:, 0:D].rearrange("p (h e) -> p h e", h=H1),
                                            orstd[:].rearrange("p (h o) -> p h o", o=1).to_broadcast([P, H1, DK]), ALU.mult).then_inc(S("on_ready"), 1)
                    wait_alone(v, S("ao_psum"), i + 1)
                    inv_std(i, bank[3][:, 0:D], "ve_ao")
                    v.wait_ge(S("rstd_ao"), i + 1)
                    nc.vector.tensor_scalar(xn[:], bank[3][:, 0:D], mv[:, 0:1], rstd[:], ALU.subtract, ALU.mult).then_inc(S("aon_ready"), 1)
                    v.wait_ge(S("aon_ready"), i + 1)
                    nc.vector.tensor_tensor(xt, xt, xn[:], ALU.add).then_inc(S("x1_ready"), 1)
                    wait_alone(v, S("x1_ready"), i + 1)
                    inv_std(i, xt, "ve_x1")
                    v.wait_ge(S("rstd_x1"), i + 1)
                    nc.vector.tensor_scalar(at, xt, mv[:, 0:1], rstd[:], ALU.subtract, ALU.mult).then_inc(S("y_ready"), 1)
                    v.wait_ge(S("yss_ready"), i + 1)
                    nc.vector.tensor_scalar(ve[:], rsum[:, 0, 0:1], 1.0 / D, EPS, ALU.mult, ALU.add).then_inc(S("ve_y"), 1)
                    v.wait_ge(S("rstd_y"), i + 1)
                    nc.vector.tensor_scalar(xn[:], at, rstd[:], None, ALU.mult).then_inc(S("r_ready"), 1)
                    v.wait_ge(S("rT_psum"), i + 1)
            with v.Fori(0, BATCH) as b:
                with v.Fori(0, NKV) as g:
                    n = b * NKV + g
                    for t in range(2):
                        cols = slice(t * HALF, (t + 1) * HALF)
                        v.wait_ge(S("khi_ready"), n * 2 + t + 1)
                        v.wait_ge(S("vT_ready"), n * 2 + t + 1)
                        for u in range(2):
                            ins = nc.vector.tensor_tensor(klo[u * DH:(u + 1) * DH, cols], wide[0:DH, t, :],
                                                          khi[0:DH, cols].bitcast(F32), ALU.subtract)
                        ins.then_inc(S("klo_ready"), 1)
                    for m in range(4):
                        v.wait_ge(S("qhi_ready"), n * 4 + m + 1)
                        for u in range(2):
                            hi = qhl[0:DH, 2 * (m // 2) + u, (m % 2) * HALF:(m % 2 + 1) * HALF]
                            lo = qhl[DH:P, 2 * (m // 2) + u, (m % 2) * HALF:(m % 2 + 1) * HALF]
                            ins = nc.vector.scalar_tensor_tensor(out=lo, in0=wide[u * DH:(u + 1) * DH, (2 + m) % 4, :], scalar=DH ** -0.5,
                                                                 in1=hi.bitcast(F32), op0=ALU.mult, op1=ALU.subtract)
                        ins.then_inc(S("qlo_ready"), 1)
                    v.wait_ge(S("v2_psum"), n + 1)
                    nc.vector.tensor_copy(vt[:], bank[3][:].rearrange("p (t d) -> p t d", t=TB)).then_inc(S("v2_ready"), 1)

                    def evac_pT(ct, m):
                        j = ct * (ct + 1) // 2 + m
                        if j % 2 == 1:
                            v.wait_ge(S("pT_psum"), n * 36 + j + 1)
                            nc.vector.tensor_copy(pT[1][:], bank[1][:]).then_inc(S("pT_odd"), 1)

                    for ct in range(TB + 1):
                        for h in range(G):
                            if ct < TB:
                                c = ct * G + h
                                w = (ct + 1) * P
                                v.wait_ge(S("scores2"), n * (TB * G) + c + 1)
                                if ct >= 2:
                                    v.wait_ge(S("probs_ready"), n * (TB * G) + c - 2 * G + 1)
                                nc.vector.tensor_reduce(nmax[:, ct % 2, h:h + 1],
                                                        wide[:, 2 * (h % 2):2 * (h % 2) + 2, :].rearrange("p a b -> p (a b)")[:, 0:w],
                                                        AX.X, ALU.max, negate=True).then_inc(S("nmax_ready"), 1)
                            if ct > 0:
                                for m in pairs_of(ct - 1, h):
                                    evac_pT(ct - 1, m)
                            if ct < TB:
                                v.wait_ge(S("exp_done"), n * (TB * G) + c + 1)
                                nc.vector.reciprocal(rinv[:, ct % 2, h:h + 1], rsum[:, ct % 2, h:h + 1]).then_inc(S("rinv_ready"), 1)
                        if ct > 0:
                            v.wait_ge(S("proj2"), n * TB + ct)
                            at = acc[:, bass.ds(b * TB + (ct - 1), 1)].rearrange("p o d -> p (o d)")
                            nc.vector.tensor_tensor(at, bank[3][:, 0:D], at, ALU.add).then_inc(S("acc_done"), 1)
            v.wait_ge(S("acc_done"), BATCH * NKV * TB)
            with v.Fori(0, NT) as i:
                at = acc[:, bass.ds(i, 1)]
                v.wait_ge(S("hss_ready"), i + 1)
                nc.vector.tensor_scalar(ve[:], rsum[:, 0, 0:1], 1.0 / D, EPS, ALU.mult, ALU.add).then_inc(S("ve_h"), 1)
                v.wait_ge(S("rstd_h"), i + 1)
                nc.vector.tensor_scalar(xn[:], at, rstd[:], None, ALU.mult).then_inc(S("t_ready"), 1)
                v.wait_ge(S("tT_ready"), i + 1)
                nc.vector.tensor_copy(rT_all[:, :, bass.ds(i * P, P)], xnT[:]).then_inc(S("tT_copied"), 1)
                v.wait_ge(S("logits_psum"), i + 1)
                nc.vector.tensor_reduce(nmax[:, 0, 0:1], bank[1][:, 0:E], AX.X, ALU.max, negate=True).then_inc(S("lmax_ready"), 1)
                v.wait_ge(S("gexp_ready"), i + 1)
                nc.vector.reciprocal(rinv[:, 0, 0:1], rsum[:, 0, 1:2]).then_inc(S("gsum_inv"), 1)
                v.wait_ge(S("gsum_inv"), i + 1)
                nc.vector.tensor_scalar(ove[:, 0:E], oss[:, 0:E], rinv[:, 0, 0:1], None, ALU.mult).then_inc(S("gprobs"), 1)
                wait_alone(v, S("gprobs"), i + 1)
                nc.vector.max(top[:], ove[:, 0:E]).then_inc(S("top_ready"), 1)
                wait_alone(v, S("top_ready"), i + 1)
                nc.vector.max_index(topi[:], top[:], ove[:, 0:E]).then_inc(S("topi_ready"), 1)
                nc.vector.tensor_tensor(rinv[:, 0, 1:2], top[:, 0:1], top[:, 1:2], ALU.add).then_inc(S("top_sum"), 1)
                v.wait_ge(S("topi_ready"), i + 1)
                nc.vector.tensor_copy(topf[:], topi[:]).then_inc(S("topf_ready"), 1)
                v.wait_ge(S("top_sum"), i + 1)
                nc.vector.reciprocal(rinv[:, 0, 2:3], rinv[:, 0, 1:2]).then_inc(S("top_inv"), 1)
                v.wait_ge(S("top_inv"), i + 1)
                nc.vector.tensor_scalar(topw[:], top[:, 0:2], rinv[:, 0, 2:3], None, ALU.mult).then_inc(S("topw_ready"), 1)
                v.wait_ge(S("topf_ready"), i + 1)
                v.wait_ge(S("topw_ready"), i + 1)
                nc.vector.tensor_scalar(pick[:, 0], experts[:], topf[:, 0:1], topw[:, 0:1], ALU.is_equal, ALU.mult).then_inc(S("pick"), 1)
                nc.vector.tensor_scalar(pick[:, 1], experts[:], topf[:, 1:2], topw[:, 1:2], ALU.is_equal, ALU.mult).then_inc(S("pick"), 1)
                v.wait_ge(S("pick"), 2 * i + 2)
                nc.vector.tensor_tensor(comb[:, bass.ds(i, 1)].rearrange("p o e -> p (o e)"), pick[:, 0], pick[:, 1], ALU.add).then_inc(S("comb_ready"), 1)
                v.wait_ge(S("comb_ready"), i + 1)
            with v.Fori(0, E // 2) as e2:
                for s in range(2):
                    e = e2 * 2 + s
                    nc.vector.tensor_copy(combe[:], comb[:, :, bass.ds(e, 1)].rearrange("p t o -> p (t o)")).then_inc(S("combe_ready"), 1)
                    wait_alone(v, S("combe_ready"), e + 1)
                    with v.Fori(0, NG) as tg:
                        n = e * NG + tg
                        for f in range(FB):
                            v.wait_ge(S("relu_ready"), n * FB + f + 1)
                            if f == 0:
                                v.wait_ge(S("down_psum"), n)
                            v.wait_ge(S("gate_psum"), n * FB + f + 1)
                            nc.vector.tensor_tensor(gated[:, f], wide[:, 2 + f % 2, :], relu[f % 2][:], ALU.mult).then_inc(S("gated_ready"), 1)
                        v.wait_ge(S("down_psum"), n + 1)
                        for j in range(TG // P):
                            nc.vector.tensor_copy(cw[:, j:j + 1], combe[:, bass.ds(tg * (TG // P) + j, 1)]).then_inc(S("cw_ready"), 1)
                        v.wait_ge(S("cw_ready"), (n + 1) * (TG // P))
                        for j in range(TG // P):
                            at = acc[:, bass.ds(tg * (TG // P) + j, 1)].rearrange("p o d -> p (o d)")
                            nc.vector.scalar_tensor_tensor(out=at, in0=bank[j // 2][:, (j % 2) * D:(j % 2 + 1) * D], scalar=cw[:, j:j + 1],
                                                           in1=at, op0=ALU.mult, op1=ALU.add).then_inc(S("down_added"), 1)
                        v.wait_ge(S("down_added"), (n + 1) * (TG // P))
            with v.Fori(0, NT) as i:
                xt = x_all[:, bass.ds(i, 1)]
                at = acc[:, bass.ds(i, 1)]
                inv_std(i, at, "ve_f")
                v.wait_ge(S("rstd_f"), i + 1)
                nc.vector.tensor_scalar(xn[:], at, mv[:, 0:1], rstd[:], ALU.subtract, ALU.mult).then_inc(S("fn_ready"), 1)
                v.wait_ge(S("fn_ready"), i + 1)
                nc.vector.tensor_tensor(xt, xt, xn[:], ALU.add).then_inc(S("out_ready"), 1)
                v.wait_ge(S("out_ready"), i + 1)

        @block.tensor
        def _(pe):
            mm = nc.tensor.matmul
            pe.wait_ge(S("constants_ready"), 12)
            pe.wait_ge(S("fdiag_ready"), 1)
            for n in range(4):
                pe.wait_ge(S("fT_ready"), n)
                nc.tensor.transpose(bank[0][:, 0:P], fdiag[:, n].rearrange("p h e -> p (h e)"), ident[:]).then_inc(S("fT_psum"), 1)
            pe.wait_ge(S("wnat_loaded"), 64)
            pe.wait_ge(S("fT_ready"), 4)
            for n in range(4):
                for k in range(KB):
                    pe.wait_ge(S("wfeat_ready"), n * KB + k)
                    for f in range(KB):
                        ins = mm(bank[0][:, f * P:(f + 1) * P], wnat[:, n // 2, f, k * P:(k + 1) * P], fdiagT[:, n], start=True, stop=True)
                    ins.then_inc(S("wfeat_psum"), 1)
            pe.wait_ge(S("wfeat_ready"), 4 * KB)
            for w, name in ((2, "wvT"), (3, "woT")):
                for k in range(KB):
                    pe.wait_ge(S("wvT_ready"), k if w == 2 else KB)
                    if w == 3:
                        pe.wait_ge(S("woT_ready"), k)
                    for f in range(KB):
                        ins = nc.tensor.transpose(bank[0][:, f * P:(f + 1) * P], wnat[:, w, f, k * P:(k + 1) * P], ident[:])
                    ins.then_inc(S(name + "_psum"), 1)
            pe.wait_ge(S("woT_ready"), KB)
            pe.wait_ge(S("wvT_ready"), KB)

            def transpose_tile(src, i, asked, given, k_from=None):
                pe.wait_ge(S(asked), i + 1)
                for k in range(KB):
                    piece = src[:, k * P:(k + 1) * P] if k_from is None else src[:, k]
                    ins = nc.tensor.transpose(bank[0][:, k * P:(k + 1) * P], piece, ident[:])
                ins.then_inc(S(given), 1)

            with pe.Fori(0, BATCH) as b, pe.Fori(0, TB) as tt:
                i = b * TB + tt
                pe.wait_ge(S("rT_ready"), i)
                transpose_tile(xn, i, "xn_ready", "xnT_psum")
                pe.wait_ge(S("xnT_ready"), i + 1)
                pe.wait_ge(S("on_ready"), i)
                for n, name in ((0, "q"), (2, "k")):
                    if n == 2:
                        pe.wait_ge(S("kvt_ready"), i)
                    for w in range(2):
                        for f in range(KB):
                            for k in range(KB):
                                ins = mm(bank[1 + n // 2][:, w * D + f * P:w * D + (f + 1) * P], wfeat[:, n + w, k, f * P:(f + 1) * P],
                                         xnT[:, k], start=(k == 0), stop=(k == KB - 1))
                    ins.then_inc(S(name + "_psum"), 1)
                pe.wait_ge(S("aon_ready"), i)
                for k in range(KB):
                    ins = mm(bank[3][:, 0:D], xnT[:, k], wvT[:, k], start=(k == 0), stop=(k == KB - 1))
                ins.then_inc(S("v_psum"), 1)
                transpose_tile(kT, i, "kT_ready", "ktok_psum", 1)
                pe.wait_ge(S("qx_ready"), i + 1)
                pe.wait_ge(S("sm_ready"), i)
                for k in range(KB):
                    for j in range(2):
                        ins = mm(wide[:, 2 * k + j, :], kT[:, k], qx[:, k, j * 4:(j + 1) * 4].rearrange("p h c -> p (h c)"), start=True, stop=True)
                ins.then_inc(S("scores1"), 1)
                pe.wait_ge(S("ktok_ready"), i + 1)
                pe.wait_ge(S("v_ready"), i + 1)
                for k in range(KB):
                    ins = mm(bank[2][:, k * P:(k + 1) * P], ktok[:, k * P:(k + 1) * P], vtok[:, k * P:(k + 1) * P], start=True, stop=True)
                ins.then_inc(S("kv_psum"), 1)
                pe.wait_ge(S("state_ready"), i)
                pe.wait_ge(S("state_clear"), b + 1)
                pe.wait_ge(S("sm_ready"), i + 1)
                for k in range(KB):
                    mm(bank[1][:, k * P:(k + 1) * P], qT[:, k], state[:, k], start=(k == 0), stop=False, skip_group_check=True)
                for h in range(H1):
                    ins = mm(bank[1][:, h * DK:(h + 1) * DK], sm[:, h], vtok[:, h * DK:(h + 1) * DK], start=False, stop=True,
                             skip_group_check=True)
                ins.then_inc(S("o_psum"), 1)
                transpose_tile(on, i, "on_ready", "onT_psum")
                pe.wait_ge(S("onT_ready"), i + 1)
                for k in range(KB):
                    ins = mm(bank[3][:, 0:D], onT[:, k], woT[:, k], start=(k == 0), stop=(k == KB - 1))
                ins.then_inc(S("ao_psum"), 1)
                transpose_tile(xn, i, "r_ready", "rT_psum")

            pe.wait_ge(S("wo2_loaded"), 16 * 2 * NKV)
            pe.wait_ge(S("rT_ready"), NT)
            with pe.Fori(0, BATCH) as b:
                with pe.Fori(0, NKV) as g:
                    n = b * NKV + g
                    pe.wait_ge(S("wq_loaded"), 16 * n + 16)
                    pe.wait_ge(S("wk_loaded"), 16 * n + 16)
                    pe.wait_ge(S("wv_loaded"), 16 * n + 16)
                    for m in range(6):
                        t = m if m < 2 else (m - 2) % 2
                        if m == 0:
                            pe.wait_ge(S("exp_done"), n * (TB * G))
                            pe.wait_ge(S("v2_ready"), n)
                        if m >= 4:
                            pe.wait_ge(S("klo_ready"), n * 2 + m - 3)
                        for k in range(KB):
                            w = wkv_g[:, k] if m < 2 else wq_g[:, k, (m - 2) // 2 * P:((m - 2) // 2 + 1) * P]
                            ins = mm(wide[:, m % 4, :], w, rT_all[:, k, bass.ds(b * SEQ + t * HALF, HALF)], start=(k == 0), stop=(k == KB - 1))
                        ins.then_inc(S("projected"), 1)
                    wait_alone(pe, S("vT_ready"), n * 2 + 2)
                    wait_alone(pe, S("acc_done"), n * TB)
                    for t in range(TB):
                        ins = nc.tensor.transpose(bank[3][:, t * DH:(t + 1) * DH], vT[:, t * P:(t + 1) * P], ident[0:DH, 0:DH])
                    ins.then_inc(S("v2_psum"), 1)
                    pe.wait_ge(S("klo_ready"), n * 2 + 2)
                    pe.wait_ge(S("qlo_ready"), n * 4 + 4)
                    pe.wait_ge(S("v2_ready"), n + 1)

                    def score(ct, h):
                        c = ct * G + h
                        if c >= 2:
                            pe.wait_ge(S("exp_done"), n * (TB * G) + c - 1)
                        w = (ct + 1) * P
                        for lo in range(0, w, 512):
                            hi = min(w, lo + 512)
                            dst = wide[:, 2 * (h % 2) + lo // 512, 0:hi - lo]
                            q = qhl[:, h, ct * P:(ct + 1) * P]
                            mm(dst, q, khi[:, lo:hi], start=True, stop=False)
                            if hi == w:
                                mm(dst[:, w - P - lo:w - lo], identb[:], above[:], start=False, stop=False)
                            ins = mm(dst, q, klo[:, lo:hi], start=False, stop=True)
                        ins.then_inc(S("scores2"), 1)

                    def weigh(ct, m):
                        j = ct * (ct + 1) // 2 + m
                        pe.wait_ge(S("pT_odd" if j % 2 else "pT_even"), n * 18 + j // 2)
                        for h in range(G):
                            ins = nc.tensor.transpose(bank[j % 2][:, h * P:(h + 1) * P], probs[:, ct % 2, h, m * P:(m + 1) * P], ident[:])
                        ins.then_inc(S("pT_psum"), 1)

                    def values(ct, m):
                        j = ct * (ct + 1) // 2 + m
                        pe.wait_ge(S("pT_odd" if j % 2 else "pT_even"), n * 18 + j // 2 + 1)
                        if m == 0:
                            pe.wait_ge(S("oT_ready"), n * TB + ct)
                        for u in range(2):
                            ins = mm(bank[2][u * DH:(u + 1) * DH, 0:2 * P], vt[:, m], pT[j % 2][:, u * 2 * P:(u + 1) * 2 * P],
                                     start=(m == 0), stop=(m == ct))
                        if m == ct:
                            ins.then_inc(S("o2_psum"), 1)

                    for ct in range(TB + 1):
                        before = []
                        for h in range(G):
                            if ct < TB:
                                score(ct, h)
                            if ct > 0:
                                if h == 0:
                                    pe.wait_ge(S("probs_ready"), n * (TB * G) + ct * G)
                                for m in pairs_of(ct - 1, h):
                                    weigh(ct - 1, m)
                                    if before:
                                        values(*before.pop())
                                    before.append((ct - 1, m))
                        if ct > 0:
                            values(*before.pop())
                            pe.wait_ge(S("oT_ready"), n * TB + ct)
                            pe.wait_ge(S("acc_done"), n * TB + ct - 1)
                            for j in range(2):
                                ins = mm(bank[3][:, 0:D], oT[:, j], wo2[:, bass.ds(g, 1), j].rearrange("p o d -> p (o d)"), start=(j == 0), stop=(j == 1))
                            ins.then_inc(S("proj2"), 1)

            with pe.Fori(0, NT) as i:
                pe.wait_ge(S("tT_ready"), i)
                transpose_tile(xn, i, "t_ready", "tT_psum")
                pe.wait_ge(S("tT_ready"), i + 1)
                pe.wait_ge(S("gexp_ready"), i)
                for k in range(KB):
                    ins = mm(bank[1][:, 0:E], xnT[:, k], gate[:, k], start=(k == 0), stop=(k == KB - 1))
                ins.then_inc(S("logits_psum"), 1)
            pe.wait_ge(S("tT_copied"), NT)
            pe.wait_ge(S("gexp_ready"), NT)
            with pe.Fori(0, E // 2) as e2:
                for s in range(2):
                    for w in ("w1", "w3", "w2"):
                        wait_alone(pe, S(f"{w}_loaded{s}"), 16 * e2 + 16)
                    with pe.Fori(0, NG) as tg:
                        n = (e2 * 2 + s) * NG + tg
                        for f in range(FB):
                            if f >= 2:
                                pe.wait_ge(S("gated_ready"), n * FB + f - 1)
                            else:
                                pe.wait_ge(S("gated_ready"), n * FB)
                            for slot, w, name in ((0, w1_e[s], "up_psum"), (2, w3_e[s], "gate_psum")):
                                for k in range(KB):
                                    ins = mm(wide[:, slot + f % 2, :], w[:, k, f * P:(f + 1) * P], rT_all[:, k, bass.ds(tg * TG, TG)],
                                             start=(k == 0), stop=(k == KB - 1))
                                ins.then_inc(S(name), 1)
                        pe.wait_ge(S("gated_ready"), n * FB + FB)
                        pe.wait_ge(S("down_added"), n * (TG // P))
                        for j in range(TG // P):
                            for f in range(FB):
                                ins = mm(bank[j // 2][:, (j % 2) * D:(j % 2 + 1) * D], gated[:, f, j * P:(j + 1) * P], w2_e[s][:, f],
                                         start=(f == 0), stop=(f == FB - 1))
                        ins.then_inc(S("down_psum"), 1)


_INS = ["L0_attn_x", "L0_attn_wq", "L0_attn_wk", "L0_attn_wv", "L0_attn_wo", "L0_attn_fq1_w", "L0_attn_fq1_b", "L0_attn_fq2_w",
        "L0_attn_fq2_b", "L0_attn_fk1_w", "L0_attn_fk1_b", "L0_attn_fk2_w", "L0_attn_fk2_b", "L0_attn_norm_w", "L0_ffn_ln1_w",
        "L0_ffn_wq", "L0_ffn_wk", "L0_ffn_wv", "L0_ffn_wo", "L0_ffn_ln2_w", "L0_ffn_gate_w", "L0_ffn_w1", "L0_ffn_w2", "L0_ffn_w3"]


def kernel(**inputs):
    import numpy as _np
    import concourse.bacc as _bacc
    from concourse.bass_utils import run_bass_kernel_spmd as _run

    nc = _bacc.Bacc("TRN2", target_bir_lowering=False, num_devices=1)
    arrays, aps = {}, {}
    for name in _INS:
        x = _np.ascontiguousarray(inputs[name])
        arrays[f"in_{name}"] = x
        aps[name] = nc.dram_tensor(f"in_{name}", x.shape, mybir.dt.from_np(x.dtype), kind="ExternalInput").ap()
    out = nc.dram_tensor("out_0", (BATCH, SEQ, D), F32, kind="ExternalOutput").ap()
    build(nc, aps, out)
    r = _run(nc, [arrays], core_ids=[0])
    return r.results[0]["out_0"]
```

```python
from contextlib import ExitStack

import concourse.bass as bass
from concourse import mybir

F32 = mybir.dt.float32
F32R = mybir.dt.float32r
BF16 = mybir.dt.bfloat16
U32 = mybir.dt.uint32
ALU = mybir.AluOpType
ACT = mybir.ActivationFunctionType
AX = mybir.AxisListType

P = 128
D = 256
KB = D // P
BATCH, SEQ = 2, 1024
NT = BATCH * SEQ // P
TB = SEQ // P
H1, DK = 16, 16
HB = P // DK
NH, NKV, DH = 32, 8, 64
G = NH // NKV
E, F = 8, 1024
FB = F // P
TOPK = 2
NS = TOPK * NT + E - 1
UR = 3
assert NS % UR == 0
HALF = SEQ // 2
PAIRS = TB * (TB + 1) // 2
EPS = 1e-5
MASKED = -1e30


NCONST = 20
ROUTED = 12


def rounds():
    order = []
    for ct in range(TB + 2):
        for h in range(G):
            tile, part = (ct - 1, h - 1) if h else (ct - 2, G - 1)
            live = 0 <= tile < TB
            blocks = [(tile, m) for m in range((tile + 1) * part // G, (tile + 1) * (part + 1) // G)] if live else []
            order.append(((ct, h) if ct < TB else None, blocks, tile if live and part == G - 1 else None))
    complete = [x[2] for x in order]
    return [(*x, late, later) for x, late, later in zip(order, [None] + complete, [None, None] + complete)]


def evacuates(j):
    return "vector" if j % 4 == 3 else "scalar"


def pair(ct, m):
    return ct * (ct + 1) // 2 + m


def build(nc, a, out):
    ctx = ExitStack()
    with ctx:
        def sb(name, shape, dt=F32):
            return ctx.enter_context(nc.sbuf_tensor(name, shape, dt))

        def wait_alone(engine, sem, value):
            value = engine.to_reg(value)
            engine.wait_ge(S("constants_ready"), NCONST)
            engine.wait_ge(sem, value)

        sems = {}

        def S(name):
            if name not in sems:
                sems[name] = ctx.enter_context(nc.semaphore(name))
            return sems[name]

        bank = [ctx.enter_context(nc.psum_tensor(f"bank{i}", [P, 512], F32)) for i in range(4)]
        wide = ctx.enter_context(nc.psum_tensor("wide", [P, 4, 512], F32))

        x_all = sb("x_all", [P, NT, D])
        acc = sb("acc", [P, NT, D])
        rT_all = sb("rT_all", [P, KB, NT * P])
        wo2 = sb("wo2", [P, NKV, 2, D])
        ident = sb("ident", [P, P])
        identb = sb("identb", [P, P], BF16)
        tri = sb("tri", [P, P])
        above = sb("above", [P, P], BF16)
        headmask = sb("headmask", [P, HB])
        experts = sb("experts", [P, E])
        neghalf = sb("neghalf", [P, H1])
        arena = sb("arena", [P, UR * 3 * KB * F])

        def part(at, n, pattern, **dims):
            return arena[:, at:at + n].rearrange(pattern, **dims)

        w_size = KB * F
        w1_e = [part((3 * u) * w_size, w_size, "p (k f) -> p k f", k=KB) for u in range(UR)]
        w3_e = [part((3 * u + 1) * w_size, w_size, "p (k f) -> p k f", k=KB) for u in range(UR)]
        w2_e = [part((3 * u + 2) * w_size, w_size, "p (f d) -> p f d", f=FB) for u in range(UR)]
        wnat = part(0, 4 * KB * D, "p (w k d) -> p w k d", w=4, k=KB)
        fnat = sb("fnat", [P, 4, DK])
        fdiag = sb("fdiag", [P, 4, HB, DK])
        fdiagT = sb("fdiagT", [P, 4, P])
        wfeat = part(4 * KB * D, 4 * KB * D, "p (w k d) -> p w k d", w=4, k=KB)
        wvT = part(8 * KB * D, KB * D, "p (k d) -> p k d", k=KB)
        woT = part(9 * KB * D, KB * D, "p (k d) -> p k d", k=KB)
        fbias = sb("fbias", [P, 4])
        fbias_q = sb("fbias_q", [P, 1])
        normw = sb("normw", [P, 1])
        ln1 = sb("ln1", [P, KB])
        ln2 = sb("ln2", [P, KB])
        gate = sb("gate", [P, KB, E])
        st6 = sb("st6", [P, 6])
        mv = sb("mv", [P, 2])
        ve = sb("ve", [P, 1])
        rstd = sb("rstd", [P, 1])
        xn = sb("xn", [P, D])
        xnT = sb("xnT", [P, KB, P])
        q1s = sb("q1s", [P, KB, P])
        k1s = sb("k1s", [P, KB, P])
        qT = sb("qT", [P, KB, P])
        kT = sb("kT", [P, KB, P])
        qx = part(10 * KB * D, KB * HB * P, "p (k h c) -> p k h c", k=KB, h=HB)
        ktok = sb("ktok", [P, D])
        vtok = sb("vtok", [P, D])
        sm = part(10 * KB * D + KB * HB * P, H1 * P, "p (h c) -> p h c", c=P)
        kvt = sb("kvt", [P, KB, P])
        state = sb("state", [P, KB, P])
        osq = sb("osq", [P, D])
        oss = sb("oss", [P, H1])
        ove = sb("ove", [P, H1])
        orstd = sb("orstd", [P, H1])
        on = sb("on", [P, D])
        onT = sb("onT", [P, KB, P])
        wq_g = sb("wq_g", [P, KB, G * DH])
        wkv_g = sb("wkv_g", [P, KB, 2 * DH])
        qhl = sb("qhl", [P, G, SEQ], F32R)
        khi = sb("khi", [P, SEQ], F32R)
        klo = sb("klo", [P, SEQ], F32R)
        vT = sb("vT", [DH, SEQ])
        vt = sb("vt", [P, TB, DH])
        probs = [part(i * G * SEQ, G * SEQ, "p (h m) -> p h m", h=G) for i in range(3)]
        nmax = sb("nmax", [P, 3, G])
        rsum = sb("rsum", [P, 3, G])
        rinv = sb("rinv", [P, 3, G])
        pT = [part(3 * G * SEQ + i * G * P, G * P, "p (o c) -> p (o c)", o=1) for i in range(4)]
        oT = sb("oT", [P, 2, P])
        hss = sb("hss", [P, NT])
        hve = sb("hve", [P, NT])
        hrstd = sb("hrstd", [P, NT])
        hmean = sb("hmean", [P, NT, 2])
        stf = sb("stf", [P, NT, 6])
        xn2 = [xn, sb("xn_b", [P, D])]
        xnT2 = [xnT, sb("xnT_b", [P, KB, P])]
        t_all = rT_all[:].rearrange("p k n -> p (k n)").rearrange("p (t c) -> p t c", t=NT)
        glog = sb("glog", [P, NT, E])
        gmax = sb("gmax", [P, NT])
        gsum = sb("gsum", [P, NT])
        top = sb("top", [P, NT, 8])
        topi = sb("topi", [P, NT, 8], U32)
        topf = sb("topf", [P, NT, TOPK])
        topw = sb("topw", [P, NT, TOPK])
        pick = sb("pick", [P, TOPK, E, NT])
        picked = sb("picked", [P, E, NT])
        upto = sb("upto", [P, E, NT])
        place = sb("place", [P, E, NT])
        full = sb("full", [P, E, NT])
        nslots = sb("nslots", [P, E])
        endslot = sb("endslot", [P, E])
        startrow = sb("startrow", [P, E])
        prod = sb("prod", [P, TOPK, E, NT])
        row = sb("row", [P, TOPK, NT])
        rowi = sb("rowi", [P, TOPK, NT], U32)
        passed = sb("passed", [1, NS, E])
        slote = sb("slote", [1, NS])
        slotm = sb("slotm", [1, NS])
        slotei = sb("slotei", [1, NS], mybir.dt.int32)
        hundreds = sb("hundreds", [P, NT])
        slotno = sb("slotno", [1, NS])
        restart = sb("restart", [P, E, NT])
        ones = sb("ones", [P, P])
        zeros = sb("zeros", [P, D])
        spare = wo2[:].rearrange("p g j d -> p (g j d)")
        relu = [spare[:, i * 4 * P:(i + 1) * 4 * P] for i in range(2)]
        gated = spare[:, 8 * P:(8 + FB) * P].rearrange("p (f c) -> p f c", f=FB)
        xs_sb = [spare[:, (16 + KB * u) * P:(16 + KB * (u + 1)) * P] for u in range(UR)]
        sT = [spare[:, (24 + KB * u) * P:(24 + KB * (u + 1)) * P].rearrange("p (k c) -> p k c", k=KB) for u in range(UR)]
        y_sb = [sb(f"y_sb{u}", [P, D]) for u in range(UR)]
        yg = part(0, NT * TOPK * D, "p (t k d) -> p t k d", t=NT, k=TOPK)
        xs = nc.dram_tensor("xs", (NS * P, D), F32, kind="Internal").ap()
        ys = nc.dram_tensor("ys", (NS * P, D), F32, kind="Internal").ap()

        block = ctx.enter_context(nc.Block())

        @block.sync
        def _(sp):
            sp.dma_start(x_all[:], a["L0_attn_x"].rearrange("b (t p) d -> p (b t) d", p=P)).then_inc(S("x_loaded"), 16)
            for n, w in enumerate(("wq", "wk", "wv", "wo")):
                sp.dma_start(wnat[:, n], a[f"L0_attn_{w}"].rearrange("(k p) d -> p k d", p=P)).then_inc(S("wnat_loaded"), 16)
            for n, w in enumerate(("fq1", "fq2", "fk1", "fk2")):
                for h in range(HB):
                    rows = slice(h * DK, (h + 1) * DK)
                    sp.dma_start(fnat[rows, n], a[f"L0_attn_{w}_w"]).then_inc(S("small_loaded"), 16)
                    sp.dma_start(fbias[rows, n:n + 1], a[f"L0_attn_{w}_b"].rearrange("(e o) -> e o", o=1)).then_inc(S("small_loaded"), 16)
            for h in range(HB):
                sp.dma_start(normw[h * DK:(h + 1) * DK], a["L0_attn_norm_w"].rearrange("(e o) -> e o", o=1)).then_inc(S("small_loaded"), 16)
            for t, w in ((ln1, "ln1_w"), (ln2, "ln2_w")):
                for k in range(KB):
                    sp.dma_start(t[:, k:k + 1], a[f"L0_ffn_{w}"][k * P:(k + 1) * P].rearrange("(e o) -> e o", o=1)).then_inc(S("small_loaded"), 16)
            sp.dma_start(gate[:], a["L0_ffn_gate_w"].rearrange("(k p) e -> p k e", p=P)).then_inc(S("small_loaded"), 16)
            wo_v = a["L0_ffn_wo"].rearrange("(g u j d) n -> u d g j n", g=NKV, u=2, j=2)
            for u in range(2):
                for g in range(NKV):
                    sp.dma_start(wo2[u * DH:(u + 1) * DH, g], wo_v[u][:, g]).then_inc(S("wo2_loaded"), 16)
            wq_v = a["L0_ffn_wq"].rearrange("(k p) n -> p k n", p=P)
            wk_v = a["L0_ffn_wk"].rearrange("(k p) n -> p k n", p=P)
            wv_v = a["L0_ffn_wv"].rearrange("(k p) n -> p k n", p=P)
            with sp.Fori(0, BATCH) as b:
                with sp.Fori(0, NKV) as g:
                    n = b * NKV + g
                    sp.wait_ge(S("projected"), n * 6)
                    sp.dma_start(wq_g[:], wq_v[:, :, bass.ds(g * (G * DH), G * DH)]).then_inc(S("wq_loaded"), 16)
                    sp.dma_start(wkv_g[:, :, 0:DH], wk_v[:, :, bass.ds(g * DH, DH)]).then_inc(S("wk_loaded"), 16)
                    sp.dma_start(wkv_g[:, :, DH:2 * DH], wv_v[:, :, bass.ds(g * DH, DH)]).then_inc(S("wv_loaded"), 16)
            w1_v = a["L0_ffn_w1"].rearrange("e (k p) f -> p e k f", p=P)
            w3_v = a["L0_ffn_w3"].rearrange("e (k p) f -> p e k f", p=P)
            w2_v = a["L0_ffn_w2"].rearrange("e (f p) d -> p e f d", p=P)
            xs_v = xs.rearrange("(s p) d -> p s d", p=P)
            sp.wait_ge(S("slots_known"), 1)
            sp.wait_ge(S("xs_scattered"), 16 * TOPK * NT)
            with sp.Fori(0, NS // UR) as it:
                for u in range(UR):
                    sp.wait_ge(S(f"slot_done{u}"), it)
                    slot = it * UR + u
                    e = sp.value_load(slotei[0:1, bass.ds(slot, 1)], min_val=0, max_val=E - 1)
                    sp.dma_start(xs_sb[u], xs_v[:, bass.ds(slot, 1)].rearrange("p o d -> p (o d)")).then_inc(S(f"xs_loaded{u}"), 16)
                    sp.dma_start(w1_e[u], w1_v[:, bass.ds(e, 1)].rearrange("p o k f -> p (o k) f")).then_inc(S(f"w1_loaded{u}"), 16)
                    sp.dma_start(w3_e[u], w3_v[:, bass.ds(e, 1)].rearrange("p o k f -> p (o k) f")).then_inc(S(f"w3_loaded{u}"), 16)
                    sp.dma_start(w2_e[u], w2_v[:, bass.ds(e, 1)].rearrange("p o f d -> p (o f) d")).then_inc(S(f"w2_loaded{u}"), 16)
            sp.wait_ge(S("slot_done0"), NS // UR)
            sp.dma_start(xs_sb[0], xs_v[:, NS - 1]).then_inc(S("xs_loaded0"), 16)
            out_v = out.rearrange("b (t p) d -> p (b t) d", p=P)
            with sp.Fori(0, NT) as i:
                sp.wait_ge(S("out_ready"), i + 1)
                sp.dma_start(out_v[:, bass.ds(i, 1)], x_all[:, bass.ds(i, 1)]).then_inc(S("stored"), 16)
            sp.wait_ge(S("stored"), 16 * NT)

        @block.gpsimd
        def _(gp):
            nc.gpsimd.memset(ident[:], 0.0).then_inc(S("constants_ready"), 1)
            nc.gpsimd.memset(tri[:], 1.0).then_inc(S("constants_ready"), 1)
            nc.gpsimd.memset(above[:], 0.0).then_inc(S("constants_ready"), 1)
            nc.gpsimd.memset(headmask[:], 1.0).then_inc(S("constants_ready"), 1)
            nc.gpsimd.memset(neghalf[:], -0.5).then_inc(S("constants_ready"), 1)
            nc.gpsimd.iota(experts[:], [[1, E]], base=0, channel_multiplier=0,
                           allow_small_or_imprecise_dtypes=True).then_inc(S("constants_ready"), 1)
            nc.gpsimd.iota(hundreds[:], [[P, NT]], base=0, channel_multiplier=0,
                           allow_small_or_imprecise_dtypes=True).then_inc(S("constants_ready"), 1)
            nc.gpsimd.iota(slotno[:], [[1, NS]], base=0, channel_multiplier=0,
                           allow_small_or_imprecise_dtypes=True).then_inc(S("constants_ready"), 1)
            nc.gpsimd.memset(ones[:], 1.0).then_inc(S("constants_ready"), 1)
            nc.gpsimd.memset(zeros[:], 0.0).then_inc(S("constants_ready"), 1)
            nc.gpsimd.memset(restart[:], 1.0).then_inc(S("constants_ready"), 1)
            nc.gpsimd.memset(glog[:], 0.0).then_inc(S("constants_ready"), 1)
            nc.gpsimd.memset(hmean[:], 0.0).then_inc(S("constants_ready"), 1)
            gp.wait_ge(S("constants_ready"), 13)
            nc.gpsimd.affine_select(out=ident[:], in_=ident[:], compare_op=ALU.not_equal, fill=1.0, base=0,
                                    pattern=[[-1, P]], channel_multiplier=1).then_inc(S("constants_ready"), 1)
            nc.gpsimd.affine_select(out=tri[:], in_=tri[:], compare_op=ALU.is_ge, fill=0.0, base=0,
                                    pattern=[[1, P]], channel_multiplier=-1).then_inc(S("constants_ready"), 1)
            nc.gpsimd.affine_select(out=above[:], in_=above[:], compare_op=ALU.is_ge, fill=MASKED, base=0,
                                    pattern=[[-1, P]], channel_multiplier=1).then_inc(S("constants_ready"), 1)
            nc.gpsimd.affine_select(out=headmask[:], in_=headmask[:], compare_op=ALU.is_ge, fill=0.0, base=0,
                                    pattern=[[-DK, HB]], channel_multiplier=1).then_inc(S("constants_ready"), 1)
            nc.gpsimd.memset(restart[:, :, 0:1], 0.0).then_inc(S("constants_ready"), 1)
            gp.wait_ge(S("constants_ready"), 18)
            nc.gpsimd.affine_select(out=headmask[:], in_=headmask[:], compare_op=ALU.is_ge, fill=0.0, base=DK - 1,
                                    pattern=[[DK, HB]], channel_multiplier=-1).then_inc(S("constants_ready"), 1)
            nc.gpsimd.tensor_copy(identb[:], ident[:]).then_inc(S("constants_ready"), 1)
            gp.wait_ge(S("constants_ready"), NCONST)
            gp.wait_ge(S("small_loaded"), 16 * (16 * 4 + HB + 2 * KB + 1))
            for n in range(4):
                ins = nc.gpsimd.tensor_tensor(fdiag[:, n], fnat[:, n:n + 1, :].to_broadcast([P, HB, DK]),
                                              headmask[:].rearrange("p (h o) -> p h o", o=1).to_broadcast([P, HB, DK]), ALU.mult)
            ins.then_inc(S("fdiag_ready"), 1)

            def power(i, n, dst, src, asked, given):
                gp.wait_ge(S(asked), i + 1)
                nc.gpsimd.tensor_tensor(dst, src, neghalf[:, 0:n], ALU.pow).then_inc(S(given), 1)

            with gp.Fori(0, NT) as i:
                power(i, 1, rstd[:], ve[:], "ve_x", "rstd_x")
                gp.wait_ge(S("qT_ready"), i + 1)
                gp.wait_ge(S("scores1"), i)
                for k in range(KB):
                    ins = nc.gpsimd.tensor_tensor(
                        qx[:, k], qT[:, k:k + 1, :].to_broadcast([P, HB, P]),
                        headmask[:].rearrange("p (h o) -> p h o", o=1).to_broadcast([P, HB, P]), ALU.mult)
                ins.then_inc(S("qx_ready"), 1)
                power(i, H1, orstd[:], ove[:], "ve_o", "rstd_o")
                power(i, 1, rstd[:], ve[:], "ve_ao", "rstd_ao")
                power(i, 1, rstd[:], ve[:], "ve_x1", "rstd_x1")
                power(i, 1, rstd[:], ve[:], "ve_y", "rstd_y")
            gp.dma_start(xs.rearrange("(s p) d -> p s d", p=P), zeros[:].rearrange("p (o d) -> p o d", o=1).to_broadcast([P, NS, D])).then_inc(S("xs_zeroed"), 16)
            power(0, NT, hrstd[:], hve[:], "ve_h", "rstd_h")
            with gp.Fori(0, NT // 2) as i2:
                for q in range(2):
                    gp.wait_ge(S("t_ready"), i2 * 2 + q + 1)
                    nc.gpsimd.tensor_copy(t_all[:, bass.ds(i2 * 2 + q, 1)].rearrange("p o d -> p (o d)"), xn2[q][:]).then_inc(S("t_kept"), 1)
            gp.wait_ge(S("t_kept"), NT)
            gp.wait_ge(S("rows_known"), 1)
            gp.wait_ge(S("xs_zeroed"), 16)
            for t in range(NT):
                for k in range(TOPK):
                    nc.gpsimd.indirect_dma_start(out=xs, out_offset=bass.IndirectOffsetOnAxis(ap=rowi[:, k, t:t + 1], axis=0),
                                                 in_=t_all[:, t], in_offset=None).then_inc(S("xs_scattered"), 16)
            ys_v = ys.rearrange("(s p) d -> p s d", p=P)
            with gp.Fori(0, NS // UR) as it:
                for u in range(UR):
                    gp.wait_ge(S(f"y_ready{u}"), it + 1)
                    gp.dma_start(ys_v[:, bass.ds(it * UR + u, 1)].rearrange("p o d -> p (o d)"), y_sb[u][:]).then_inc(S(f"ys_stored{u}"), 16)
            for u in range(UR):
                gp.wait_ge(S(f"ys_stored{u}"), 16 * (NS // UR))
            for t in range(NT):
                for k in range(TOPK):
                    nc.gpsimd.indirect_dma_start(out=yg[:, t, k], out_offset=None, in_=ys,
                                                 in_offset=bass.IndirectOffsetOnAxis(ap=rowi[:, k, t:t + 1], axis=0)).then_inc(S(f"gathered{t // 4}"), 16)
            power(0, NT, hrstd[:], hve[:], "ve_f", "rstd_f")

        @block.scalar
        def _(act):
            for n in range(4):
                act.wait_ge(S("fT_psum"), n + 1)
                nc.scalar.copy(fdiagT[:, n], bank[0][:, 0:P]).then_inc(S("fT_ready"), 1)
            for n in range(4):
                for k in range(KB):
                    act.wait_ge(S("wfeat_psum"), n * KB + k + 1)
                    nc.scalar.copy(wfeat[:, n, k], bank[0][:, 0:D]).then_inc(S("wfeat_ready"), 1)
            for k in range(KB):
                act.wait_ge(S("wvT_psum"), k + 1)
                nc.scalar.copy(wvT[:, k], bank[0][:, 0:D]).then_inc(S("wvT_ready"), 1)
            for k in range(KB):
                act.wait_ge(S("woT_psum"), k + 1)
                nc.scalar.activation(woT[:, k], bank[0][:, 0:D], ACT.Copy, scale=normw[:, 0:1]).then_inc(S("woT_ready"), 1)
            nc.scalar.activation(fbias_q[:], fbias[:, 0:1], ACT.Copy, scale=DK ** -0.5).then_inc(S("fbias_q_ready"), 1)
            act.wait_ge(S("fbias_q_ready"), 1)
            with act.Fori(0, NT) as i:
                act.wait_ge(S("xnT_psum"), i + 1)
                act.wait_ge(S("v_psum"), i)
                nc.scalar.copy(xnT[:], bank[0][:, 0:D].rearrange("p (k c) -> p k c", k=KB)).then_inc(S("xnT_ready"), 1)
                act.wait_ge(S("q_psum"), i + 1)
                act.wait_ge(S("qT_ready"), i)
                nc.scalar.activation(q1s[:], bank[1][:, 0:D].rearrange("p (k c) -> p k c", k=KB), ACT.Identity, bias=fbias_q[:, 0:1],
                                     scale=DK ** -0.5).then_inc(S("q1_ready"), 1)
                act.wait_ge(S("k_psum"), i + 1)
                act.wait_ge(S("kT_ready"), i)
                nc.scalar.activation(k1s[:], bank[2][:, 0:D].rearrange("p (k c) -> p k c", k=KB), ACT.Identity, bias=fbias[:, 2:3]).then_inc(S("k1_ready"), 1)
                act.wait_ge(S("v_psum"), i + 1)
                act.wait_ge(S("o_psum"), i)
                act.wait_ge(S("kv_psum"), i)
                nc.scalar.copy(vtok[:], bank[3][:, 0:D]).then_inc(S("v_ready"), 1)
                act.wait_ge(S("ktok_psum"), i + 1)
                nc.scalar.copy(ktok[:], bank[0][:, 0:D]).then_inc(S("ktok_ready"), 1)
                act.wait_ge(S("o_psum"), i + 1)
                act.wait_ge(S("oss_ready"), i)
                act.wait_ge(S("yss_ready"), i)
                nc.scalar.activation(osq[:], bank[1][:, 0:D], ACT.Square).then_inc(S("osq_ready"), 1)
                act.wait_ge(S("onT_psum"), i + 1)
                nc.scalar.copy(onT[:], bank[0][:, 0:D].rearrange("p (k c) -> p k c", k=KB)).then_inc(S("onT_ready"), 1)
                act.wait_ge(S("y_ready"), i + 1)
                nc.scalar.activation(osq[:], acc[:, bass.ds(i, 1)], ACT.Square, accum_out=rsum[:, 0, 0:1]).then_inc(S("yss_ready"), 1)
                act.wait_ge(S("rT_psum"), i + 1)
                for k in range(KB):
                    ins = nc.scalar.activation(rT_all[:, k, bass.ds(i * P, P)], bank[0][:, k * P:(k + 1) * P], ACT.Copy,
                                               scale=ln1[:, k:k + 1])
                ins.then_inc(S("rT_ready"), 1)
            with act.Fori(0, BATCH * NKV) as n:
                for t in range(2):
                    cols = slice(t * HALF, (t + 1) * HALF)
                    act.wait_ge(S("projected"), n * 6 + t + 1)
                    for u in range(2):
                        ins = nc.scalar.copy(khi[u * DH:(u + 1) * DH, cols], wide[0:DH, t, :])
                    ins.then_inc(S("khi_ready"), 1)
                    nc.scalar.copy(vT[:, cols], wide[DH:P, t, :]).then_inc(S("vT_ready"), 1)
                for m in range(4):
                    act.wait_ge(S("projected"), n * 6 + 2 + m + 1)
                    for u in range(2):
                        ins = nc.scalar.activation(qhl[0:DH, 2 * (m // 2) + u, (m % 2) * HALF:(m % 2 + 1) * HALF],
                                                   wide[u * DH:(u + 1) * DH, (2 + m) % 4, :], ACT.Copy, scale=DH ** -0.5)
                    ins.then_inc(S("qhi_ready"), 1)

                for score, blocks, complete, project, add in rounds():
                    for ct, m in blocks:
                        j = pair(ct, m)
                        if evacuates(j) == "scalar":
                            act.wait_ge(S("pT_psum"), n * PAIRS + j + 1)
                            nc.scalar.copy(pT[j % 4], bank[j % 2][:]).then_inc(S("pT_odd" if j % 2 else "pT_even"), 1)
                    if score:
                        ct, h = score
                        w = (ct + 1) * P
                        act.wait_ge(S("nmax_ready"), n * (TB * G) + ct * G + h + 1)
                        nc.scalar.activation(probs[ct % 3][:, h, 0:w],
                                             wide[:, 2 * (h % 2):2 * (h % 2) + 2, :].rearrange("p a b -> p (a b)")[:, 0:w],
                                             ACT.Exp, bias=nmax[:, ct % 3, h:h + 1],
                                             accum_out=rsum[:, ct % 3, h:h + 1]).then_inc(S("exp_done"), 1)
                    if complete is not None:
                        act.wait_ge(S("o2_psum"), n * TB + complete + 1)
                        nc.scalar.copy(oT[:], bank[2][:, 0:2 * P].rearrange("p (j c) -> p j c", j=2)).then_inc(S("oT_ready"), 1)
            act.wait_ge(S("acc_done"), BATCH * NKV * TB)
            with act.Fori(0, NT) as i:
                act.wait_ge(S("hss_ready"), i)
                nc.scalar.activation(osq[:], acc[:, bass.ds(i, 1)], ACT.Square, accum_out=hss[:, bass.ds(i, 1)]).then_inc(S("hss_ready"), 1)
            with act.Fori(0, NT // 2) as i2:
                for q in range(2):
                    i = i2 * 2 + q
                    act.wait_ge(S("tT_psum"), i + 1)
                    act.wait_ge(S("logits_psum"), i2 * 2 if q == 0 else i2 * 2)
                    for k in range(KB):
                        ins = nc.scalar.activation(xnT2[q][:, k], bank[q][:, k * P:(k + 1) * P], ACT.Copy, scale=ln2[:, k:k + 1])
                    ins.then_inc(S("tT_ready"), 1)
            act.wait_ge(S("glog_ready"), 1)
            nc.scalar.activation(glog[:], glog[:], ACT.Exp).then_inc(S("gexp_ready"), 1)

            def evacuate_slot(u, n):
                act.wait_ge(S("sT_psum"), n)
                for k in range(KB):
                    ins = nc.scalar.activation(sT[u][:, k], bank[3][:, k * P:(k + 1) * P], ACT.Copy, scale=ln2[:, k:k + 1])
                ins.then_inc(S("sT_ready"), 1)

            evacuate_slot(0, 1)
            with act.Fori(0, NS // UR) as it:
                for u in range(UR):
                    slot = it * UR + u
                    for half in range(2):
                        act.wait_ge(S("up_psum"), slot * 2 + half + 1)
                        act.wait_ge(S("gated_ready"), slot * 2)
                        nc.scalar.activation(relu[half], wide[:, half, :], ACT.Relu).then_inc(S("relu_ready"), 1)
                    evacuate_slot((u + 1) % UR, slot + 2)
                    act.wait_ge(S(f"slot_done{u}"), it + 1)
                    act.wait_ge(S(f"ys_stored{u}"), 16 * it)
                    nc.scalar.copy(y_sb[u][:], bank[u][:, 0:D]).then_inc(S(f"y_ready{u}"), 1)

        @block.vector
        def _(v):
            def inv_std(i, src, asked, mean_in_mv=True):
                nc.vector.bn_stats(st6[:], src).then_inc(S(asked + "_st"), 1)
                wait_alone(v, S(asked + "_st"), i + 1)
                nc.vector.bn_aggr(mv[:], st6[:]).then_inc(S(asked + "_mv"), 1)
                v.wait_ge(S(asked + "_mv"), i + 1)
                nc.vector.tensor_scalar(ve[:], mv[:, 1:2], EPS, None, ALU.add).then_inc(S(asked), 1)

            v.wait_ge(S("x_loaded"), 16)
            with v.Fori(0, BATCH) as b:
                v.wait_ge(S("o_psum"), b * TB)
                v.wait_ge(S("state_ready"), b * TB)
                nc.vector.memset(state[:], 0.0).then_inc(S("state_clear"), 1)
                wait_alone(v, S("state_clear"), b + 1)
                with v.Fori(0, TB) as t:
                    i = b * TB + t
                    xt = x_all[:, bass.ds(i, 1)]
                    at = acc[:, bass.ds(i, 1)]
                    inv_std(i, xt, "ve_x")
                    v.wait_ge(S("rstd_x"), i + 1)
                    nc.vector.tensor_scalar(xn[:], xt, mv[:, 0:1], rstd[:], ALU.subtract, ALU.mult).then_inc(S("xn_ready"), 1)
                    v.wait_ge(S("q1_ready"), i + 1)
                    v.wait_ge(S("o_psum"), i)
                    nc.vector.scalar_tensor_tensor(out=qT[:], in0=bank[1][:, D:2 * D].rearrange("p (k c) -> p k c", k=KB), scalar=fbias[:, 1:2], in1=q1s[:],
                                                   op0=ALU.add, op1=ALU.mult).then_inc(S("qT_ready"), 1)
                    v.wait_ge(S("k1_ready"), i + 1)
                    nc.vector.scalar_tensor_tensor(out=kT[:], in0=bank[2][:, D:2 * D].rearrange("p (k c) -> p k c", k=KB), scalar=fbias[:, 3:4], in1=k1s[:],
                                                   op0=ALU.add, op1=ALU.mult).then_inc(S("kT_ready"), 1)
                    v.wait_ge(S("scores1"), i + 1)
                    nc.vector.tensor_tensor(sm[:], wide[:].rearrange("p a (h c) -> p (a h) c", c=P),
                                            tri[:].rearrange("p (o c) -> p o c", o=1).to_broadcast([P, H1, P]), ALU.mult).then_inc(S("sm_ready"), 1)
                    v.wait_ge(S("kv_psum"), i + 1)
                    v.wait_ge(S("state_ready"), i)
                    nc.vector.tensor_tensor(kvt[:].rearrange("p k (h e) -> p k h e", h=HB),
                                            bank[2][:, 0:D].rearrange("p (k h e) -> p k h e", k=KB, h=HB),
                                            headmask[:].rearrange("p (o h q) -> p o h q", o=1, q=1).to_broadcast([P, KB, HB, DK]),
                                            ALU.mult).then_inc(S("kvt_ready"), 1)
                    v.wait_ge(S("kvt_ready"), i + 1)
                    v.wait_ge(S("o_psum"), i + 1)
                    nc.vector.tensor_tensor(state[:], state[:], kvt[:], ALU.add).then_inc(S("state_ready"), 1)
                    v.wait_ge(S("osq_ready"), i + 1)
                    nc.vector.tensor_reduce(oss[:], osq[:].rearrange("p (h e) -> p h e", h=H1), AX.X, ALU.add).then_inc(S("oss_ready"), 1)
                    v.wait_ge(S("oss_ready"), i + 1)
                    nc.vector.tensor_scalar(ove[:], oss[:], 1.0 / DK, EPS, ALU.mult, ALU.add).then_inc(S("ve_o"), 1)
                    v.wait_ge(S("rstd_o"), i + 1)
                    nc.vector.tensor_tensor(on[:].rearrange("p (h e) -> p h e", h=H1), bank[1][:, 0:D].rearrange("p (h e) -> p h e", h=H1),
                                            orstd[:].rearrange("p (h o) -> p h o", o=1).to_broadcast([P, H1, DK]), ALU.mult).then_inc(S("on_ready"), 1)
                    wait_alone(v, S("ao_psum"), i + 1)
                    inv_std(i, bank[3][:, 0:D], "ve_ao")
                    v.wait_ge(S("rstd_ao"), i + 1)
                    nc.vector.tensor_scalar(xn[:], bank[3][:, 0:D], mv[:, 0:1], rstd[:], ALU.subtract, ALU.mult).then_inc(S("aon_ready"), 1)
                    v.wait_ge(S("aon_ready"), i + 1)
                    nc.vector.tensor_tensor(xt, xt, xn[:], ALU.add).then_inc(S("x1_ready"), 1)
                    wait_alone(v, S("x1_ready"), i + 1)
                    inv_std(i, xt, "ve_x1")
                    v.wait_ge(S("rstd_x1"), i + 1)
                    nc.vector.tensor_scalar(at, xt, mv[:, 0:1], rstd[:], ALU.subtract, ALU.mult).then_inc(S("y_ready"), 1)
                    v.wait_ge(S("yss_ready"), i + 1)
                    nc.vector.tensor_scalar(ve[:], rsum[:, 0, 0:1], 1.0 / D, EPS, ALU.mult, ALU.add).then_inc(S("ve_y"), 1)
                    v.wait_ge(S("rstd_y"), i + 1)
                    nc.vector.tensor_scalar(xn[:], at, rstd[:], None, ALU.mult).then_inc(S("r_ready"), 1)
                    v.wait_ge(S("rT_psum"), i + 1)
            with v.Fori(0, BATCH) as b:
                with v.Fori(0, NKV) as g:
                    n = b * NKV + g
                    for t in range(2):
                        cols = slice(t * HALF, (t + 1) * HALF)
                        v.wait_ge(S("khi_ready"), n * 2 + t + 1)
                        v.wait_ge(S("vT_ready"), n * 2 + t + 1)
                        for u in range(2):
                            ins = nc.vector.tensor_tensor(klo[u * DH:(u + 1) * DH, cols], wide[0:DH, t, :],
                                                          khi[0:DH, cols].bitcast(F32), ALU.subtract)
                        ins.then_inc(S("klo_ready"), 1)
                    for m in range(4):
                        v.wait_ge(S("qhi_ready"), n * 4 + m + 1)
                        for u in range(2):
                            hi = qhl[0:DH, 2 * (m // 2) + u, (m % 2) * HALF:(m % 2 + 1) * HALF]
                            lo = qhl[DH:P, 2 * (m // 2) + u, (m % 2) * HALF:(m % 2 + 1) * HALF]
                            ins = nc.vector.scalar_tensor_tensor(out=lo, in0=wide[u * DH:(u + 1) * DH, (2 + m) % 4, :], scalar=DH ** -0.5,
                                                                 in1=hi.bitcast(F32), op0=ALU.mult, op1=ALU.subtract)
                        ins.then_inc(S("qlo_ready"), 1)
                    v.wait_ge(S("v2_psum"), n + 1)
                    nc.vector.tensor_copy(vt[:], bank[3][:].rearrange("p (t d) -> p t d", t=TB)).then_inc(S("v2_ready"), 1)

                    def normalise(ct, h):
                        c = ct * G + h
                        w = (ct + 1) * P
                        v.wait_ge(S("exp_done"), n * (TB * G) + c + 1)
                        nc.vector.reciprocal(rinv[:, ct % 3, h:h + 1], rsum[:, ct % 3, h:h + 1]).then_inc(S("rinv_ready"), 1)
                        v.wait_ge(S("rinv_ready"), n * (TB * G) + c + 1)
                        nc.vector.tensor_scalar(probs[ct % 3][:, h, 0:w], probs[ct % 3][:, h, 0:w],
                                                rinv[:, ct % 3, h:h + 1], None, ALU.mult).then_inc(S("probs_ready"), 1)

                    last = None
                    for score, blocks, complete, project, add in rounds():
                        if score:
                            ct, h = score
                            w = (ct + 1) * P
                            v.wait_ge(S("scores2"), n * (TB * G) + ct * G + h + 1)
                            nc.vector.tensor_reduce(nmax[:, ct % 3, h:h + 1],
                                                    wide[:, 2 * (h % 2):2 * (h % 2) + 2, :].rearrange("p a b -> p (a b)")[:, 0:w],
                                                    AX.X, ALU.max, negate=True).then_inc(S("nmax_ready"), 1)
                        for ct, m in blocks:
                            j = pair(ct, m)
                            if evacuates(j) == "vector":
                                v.wait_ge(S("pT_psum"), n * PAIRS + j + 1)
                                nc.vector.tensor_copy(pT[j % 4], bank[1][:]).then_inc(S("pT_odd"), 1)
                        if last:
                            normalise(*last)
                        last = score
                        if add is not None:
                            v.wait_ge(S("proj2"), n * TB + add + 1)
                            at = acc[:, bass.ds(b * TB + add, 1)].rearrange("p o d -> p (o d)")
                            nc.vector.tensor_tensor(at, bank[3][:, 0:D], at, ALU.add).then_inc(S("acc_done"), 1)
            v.wait_ge(S("acc_done"), BATCH * NKV * TB)
            v.wait_ge(S("hss_ready"), NT)
            nc.vector.tensor_scalar(hve[:], hss[:], 1.0 / D, EPS, ALU.mult, ALU.add).then_inc(S("ve_h"), 1)
            v.wait_ge(S("rstd_h"), 1)
            with v.Fori(0, NT // 2) as i2:
                for q in range(2):
                    i = i2 * 2 + q
                    v.wait_ge(S("tT_psum"), i2 * 2)
                    v.wait_ge(S("t_kept"), i2 * 2)
                    nc.vector.tensor_scalar(xn2[q][:], acc[:, bass.ds(i, 1)], hrstd[:, bass.ds(i, 1)], None, ALU.mult).then_inc(S("t_ready"), 1)

            steps = [0]

            def step(ins):
                steps[0] += 1
                ins.then_inc(S("router_steps"), 1)
                v.wait_ge(S("router_steps"), steps[0])

            def over_experts(x):
                return x.rearrange("p (t o) -> p t o", o=1).to_broadcast([P, NT, E])

            v.wait_ge(S("logits_psum"), NT)
            logits = bank[2][:, 0:NT * E].rearrange("p (t e) -> p t e", t=NT)
            step(nc.vector.tensor_reduce(gmax[:], logits, AX.X, ALU.max))
            nc.vector.tensor_tensor(glog[:], logits, over_experts(gmax[:]), ALU.subtract).then_inc(S("glog_ready"), 1)
            v.wait_ge(S("gexp_ready"), 1)
            step(nc.vector.tensor_reduce(gsum[:], glog[:], AX.X, ALU.add))
            step(nc.vector.reciprocal(gsum[:], gsum[:]))
            step(nc.vector.tensor_tensor(glog[:], glog[:], over_experts(gsum[:]), ALU.mult))
            for t in range(NT):
                ins = nc.vector.max(top[:, t], glog[:, t])
            step(ins)
            for t in range(NT):
                ins = nc.vector.max_index(topi[:, t], top[:, t], glog[:, t])
            step(ins)
            step(nc.vector.tensor_copy(topf[:], topi[:, :, 0:TOPK]))
            step(nc.vector.tensor_tensor(gsum[:], top[:, :, 0], top[:, :, 1], ALU.add))
            step(nc.vector.reciprocal(gmax[:], gsum[:]))
            step(nc.vector.tensor_tensor(topw[:], top[:, :, 0:TOPK], gmax[:].rearrange("p (t o) -> p t o", o=1).to_broadcast([P, NT, TOPK]), ALU.mult))
            for k in range(TOPK):
                ins = nc.vector.tensor_tensor(pick[:, k], experts[:].rearrange("p (e o) -> p e o", o=1).to_broadcast([P, E, NT]),
                                              topf[:, :, k].rearrange("p (o t) -> p o t", o=1).to_broadcast([P, E, NT]), ALU.is_equal)
            step(ins)
            step(nc.vector.tensor_tensor(picked[:], pick[:, 0], pick[:, 1], ALU.add))
            v.wait_ge(S("ranks_psum"), 1)
            flat = "p e t -> p (e t)"
            within = bank[0][:, 0:E * NT].rearrange("p (e t) -> p e t", e=E)
            totals = bank[1][:, 0:E * NT].rearrange("p (e t) -> p e t", e=E)
            step(nc.vector.tensor_tensor_scan(upto[:].rearrange(flat), restart[:].rearrange(flat), totals.rearrange(flat), 0.0, ALU.mult, ALU.add))
            step(nc.vector.tensor_tensor(full[:], upto[:, :, NT - 1:NT].to_broadcast([P, E, NT]),
                                         hundreds[:].rearrange("p (o t) -> p o t", o=1).to_broadcast([P, E, NT]), ALU.is_gt))
            step(nc.vector.tensor_reduce(nslots[:], full[:], AX.X, ALU.add))
            step(nc.vector.tensor_tensor_scan(endslot[:], ones[:, 0:E], nslots[:], 0.0, ALU.mult, ALU.add))
            step(nc.vector.tensor_tensor(passed[:], slotno[:].rearrange("p (s o) -> p s o", o=1).to_broadcast([1, NS, E]),
                                         endslot[0:1].rearrange("p (o e) -> p o e", o=1).to_broadcast([1, NS, E]), ALU.is_ge))
            step(nc.vector.tensor_reduce(slote[:], passed[:], AX.X, ALU.add))
            step(nc.vector.tensor_scalar(slotm[:], slote[:], float(E - 1), None, ALU.min))
            nc.vector.tensor_copy(slotei[:], slotm[:]).then_inc(S("slots_known"), 1)
            step(nc.vector.tensor_tensor(startrow[:], endslot[:], nslots[:], ALU.subtract))
            step(nc.vector.tensor_tensor(place[:], upto[:], totals, ALU.subtract))
            step(nc.vector.scalar_tensor_tensor(out=place[:], in0=startrow[:].rearrange("p (e o) -> p e o", o=1).to_broadcast([P, E, NT]), scalar=float(P),
                                                in1=place[:], op0=ALU.mult, op1=ALU.add))
            step(nc.vector.tensor_tensor(place[:], within, place[:], ALU.add))
            for k in range(TOPK):
                ins = nc.vector.tensor_tensor(prod[:, k], pick[:, k], place[:], ALU.mult)
            step(ins)
            for k in range(TOPK):
                ins = nc.vector.tensor_reduce(row[:, k], prod[:, k].rearrange("p e t -> p t e"), AX.X, ALU.add)
            step(ins)
            step(nc.vector.tensor_scalar(row[:], row[:], -1.0, None, ALU.add))
            nc.vector.tensor_copy(rowi[:], row[:]).then_inc(S("rows_known"), 1)

            with v.Fori(0, NS // UR) as it:
                for u in range(UR):
                    slot = it * UR + u
                    for half in range(2):
                        v.wait_ge(S("relu_ready"), slot * 2 + half + 1)
                        v.wait_ge(S("gate_psum"), slot * 2 + half + 1)
                        nc.vector.tensor_tensor(gated[:, half * 4:half * 4 + 4].rearrange("p f c -> p (f c)"), wide[:, 2 + half, :], relu[half],
                                                ALU.mult).then_inc(S("gated_ready"), 1)
            for quarter in range(4):
                tiles = range(quarter * (NT // 4), (quarter + 1) * (NT // 4))
                v.wait_ge(S(f"gathered{quarter}"), 16 * TOPK * (NT // 4))
                for k in range(TOPK):
                    for i in tiles:
                        ins = nc.vector.scalar_tensor_tensor(out=acc[:, i], in0=yg[:, i, k], scalar=topw[:, i, k:k + 1], in1=acc[:, i],
                                                             op0=ALU.mult, op1=ALU.add)
                    ins.then_inc(S("weighed"), 1)
                    v.wait_ge(S("weighed"), TOPK * quarter + k + 1)
                for i in tiles:
                    ins = nc.vector.bn_stats(stf[:, i], acc[:, i])
                ins.then_inc(S("ve_f_st"), 1)
            v.wait_ge(S("ve_f_st"), 4)
            for i in range(NT):
                ins = nc.vector.bn_aggr(hmean[:, i], stf[:, i])
            ins.then_inc(S("ve_f_mv"), 1)
            v.wait_ge(S("ve_f_mv"), 1)
            nc.vector.tensor_scalar(hve[:], hmean[:, :, 1], EPS, None, ALU.add).then_inc(S("ve_f"), 1)
            v.wait_ge(S("rstd_f"), 1)
            with v.Fori(0, NT) as i:
                xt = x_all[:, bass.ds(i, 1)]
                at = acc[:, bass.ds(i, 1)]
                nc.vector.tensor_scalar(at, at, hmean[:, bass.ds(i, 1), 0], hrstd[:, bass.ds(i, 1)], ALU.subtract, ALU.mult).then_inc(S("fn_ready"), 1)
                v.wait_ge(S("fn_ready"), i + 1)
                nc.vector.tensor_tensor(xt, xt, at, ALU.add).then_inc(S("out_ready"), 1)

        @block.tensor
        def _(pe):
            mm = nc.tensor.matmul
            pe.wait_ge(S("constants_ready"), NCONST)
            pe.wait_ge(S("fdiag_ready"), 1)
            for n in range(4):
                pe.wait_ge(S("fT_ready"), n)
                nc.tensor.transpose(bank[0][:, 0:P], fdiag[:, n].rearrange("p h e -> p (h e)"), ident[:]).then_inc(S("fT_psum"), 1)
            pe.wait_ge(S("wnat_loaded"), 64)
            pe.wait_ge(S("fT_ready"), 4)
            for n in range(4):
                for k in range(KB):
                    pe.wait_ge(S("wfeat_ready"), n * KB + k)
                    for f in range(KB):
                        ins = mm(bank[0][:, f * P:(f + 1) * P], wnat[:, n // 2, f, k * P:(k + 1) * P], fdiagT[:, n], start=True, stop=True)
                    ins.then_inc(S("wfeat_psum"), 1)
            pe.wait_ge(S("wfeat_ready"), 4 * KB)
            for w, name in ((2, "wvT"), (3, "woT")):
                for k in range(KB):
                    pe.wait_ge(S("wvT_ready"), k if w == 2 else KB)
                    if w == 3:
                        pe.wait_ge(S("woT_ready"), k)
                    for f in range(KB):
                        ins = nc.tensor.transpose(bank[0][:, f * P:(f + 1) * P], wnat[:, w, f, k * P:(k + 1) * P], ident[:])
                    ins.then_inc(S(name + "_psum"), 1)
            pe.wait_ge(S("woT_ready"), KB)
            pe.wait_ge(S("wvT_ready"), KB)

            def transpose_tile(src, i, asked, given, k_from=None):
                pe.wait_ge(S(asked), i + 1)
                for k in range(KB):
                    piece = src[:, k * P:(k + 1) * P] if k_from is None else src[:, k]
                    ins = nc.tensor.transpose(bank[0][:, k * P:(k + 1) * P], piece, ident[:])
                ins.then_inc(S(given), 1)

            with pe.Fori(0, BATCH) as b, pe.Fori(0, TB) as tt:
                i = b * TB + tt
                pe.wait_ge(S("rT_ready"), i)
                transpose_tile(xn, i, "xn_ready", "xnT_psum")
                pe.wait_ge(S("xnT_ready"), i + 1)
                pe.wait_ge(S("on_ready"), i)
                for n, name in ((0, "q"), (2, "k")):
                    if n == 2:
                        pe.wait_ge(S("kvt_ready"), i)
                    for w in range(2):
                        for f in range(KB):
                            for k in range(KB):
                                ins = mm(bank[1 + n // 2][:, w * D + f * P:w * D + (f + 1) * P], wfeat[:, n + w, k, f * P:(f + 1) * P],
                                         xnT[:, k], start=(k == 0), stop=(k == KB - 1))
                    ins.then_inc(S(name + "_psum"), 1)
                pe.wait_ge(S("aon_ready"), i)
                for k in range(KB):
                    ins = mm(bank[3][:, 0:D], xnT[:, k], wvT[:, k], start=(k == 0), stop=(k == KB - 1))
                ins.then_inc(S("v_psum"), 1)
                transpose_tile(kT, i, "kT_ready", "ktok_psum", 1)
                pe.wait_ge(S("qx_ready"), i + 1)
                pe.wait_ge(S("sm_ready"), i)
                for k in range(KB):
                    for j in range(2):
                        ins = mm(wide[:, 2 * k + j, :], kT[:, k], qx[:, k, j * 4:(j + 1) * 4].rearrange("p h c -> p (h c)"), start=True, stop=True)
                ins.then_inc(S("scores1"), 1)
                pe.wait_ge(S("ktok_ready"), i + 1)
                pe.wait_ge(S("v_ready"), i + 1)
                for k in range(KB):
                    ins = mm(bank[2][:, k * P:(k + 1) * P], ktok[:, k * P:(k + 1) * P], vtok[:, k * P:(k + 1) * P], start=True, stop=True)
                ins.then_inc(S("kv_psum"), 1)
                pe.wait_ge(S("state_ready"), i)
                pe.wait_ge(S("state_clear"), b + 1)
                pe.wait_ge(S("sm_ready"), i + 1)
                for k in range(KB):
                    mm(bank[1][:, k * P:(k + 1) * P], qT[:, k], state[:, k], start=(k == 0), stop=False, skip_group_check=True)
                for h in range(H1):
                    ins = mm(bank[1][:, h * DK:(h + 1) * DK], sm[:, h], vtok[:, h * DK:(h + 1) * DK], start=False, stop=True,
                             skip_group_check=True)
                ins.then_inc(S("o_psum"), 1)
                transpose_tile(on, i, "on_ready", "onT_psum")
                pe.wait_ge(S("onT_ready"), i + 1)
                for k in range(KB):
                    ins = mm(bank[3][:, 0:D], onT[:, k], woT[:, k], start=(k == 0), stop=(k == KB - 1))
                ins.then_inc(S("ao_psum"), 1)
                transpose_tile(xn, i, "r_ready", "rT_psum")

            pe.wait_ge(S("wo2_loaded"), 16 * 2 * NKV)
            pe.wait_ge(S("rT_ready"), NT)
            with pe.Fori(0, BATCH) as b:
                with pe.Fori(0, NKV) as g:
                    n = b * NKV + g
                    pe.wait_ge(S("wq_loaded"), 16 * n + 16)
                    pe.wait_ge(S("wk_loaded"), 16 * n + 16)
                    pe.wait_ge(S("wv_loaded"), 16 * n + 16)
                    for m in range(6):
                        t = m if m < 2 else (m - 2) % 2
                        if m == 0:
                            pe.wait_ge(S("exp_done"), n * (TB * G))
                            pe.wait_ge(S("v2_ready"), n)
                        if m >= 4:
                            pe.wait_ge(S("klo_ready"), n * 2 + m - 3)
                        for k in range(KB):
                            w = wkv_g[:, k] if m < 2 else wq_g[:, k, (m - 2) // 2 * P:((m - 2) // 2 + 1) * P]
                            ins = mm(wide[:, m % 4, :], w, rT_all[:, k, bass.ds(b * SEQ + t * HALF, HALF)], start=(k == 0), stop=(k == KB - 1))
                        ins.then_inc(S("projected"), 1)
                    wait_alone(pe, S("vT_ready"), n * 2 + 2)
                    wait_alone(pe, S("acc_done"), n * TB)
                    for t in range(TB):
                        ins = nc.tensor.transpose(bank[3][:, t * DH:(t + 1) * DH], vT[:, t * P:(t + 1) * P], ident[0:DH, 0:DH])
                    ins.then_inc(S("v2_psum"), 1)
                    pe.wait_ge(S("klo_ready"), n * 2 + 2)
                    pe.wait_ge(S("qlo_ready"), n * 4 + 4)
                    pe.wait_ge(S("v2_ready"), n + 1)

                    def score(ct, h):
                        c = ct * G + h
                        if c >= 2:
                            pe.wait_ge(S("exp_done"), n * (TB * G) + c - 1)
                        w = (ct + 1) * P
                        for lo in range(0, w, 512):
                            hi = min(w, lo + 512)
                            dst = wide[:, 2 * (h % 2) + lo // 512, 0:hi - lo]
                            q = qhl[:, h, ct * P:(ct + 1) * P]
                            mm(dst, q, khi[:, lo:hi], start=True, stop=False)
                            if hi == w:
                                mm(dst[:, w - P - lo:w - lo], identb[:], above[:], start=False, stop=False)
                            ins = mm(dst, q, klo[:, lo:hi], start=False, stop=True)
                        ins.then_inc(S("scores2"), 1)

                    def weigh(ct, m):
                        j = pair(ct, m)
                        pe.wait_ge(S("pT_odd" if j % 2 else "pT_even"), n * (PAIRS // 2) + j // 2)
                        if m == 0:
                            pe.wait_ge(S("probs_ready"), n * (TB * G) + (ct + 1) * G)
                        for h in range(G):
                            ins = nc.tensor.transpose(bank[j % 2][:, h * P:(h + 1) * P], probs[ct % 3][:, h, m * P:(m + 1) * P], ident[:])
                        ins.then_inc(S("pT_psum"), 1)

                    def values(ct, m):
                        j = pair(ct, m)
                        pe.wait_ge(S("pT_odd" if j % 2 else "pT_even"), n * (PAIRS // 2) + j // 2 + 1)
                        if m == 0:
                            pe.wait_ge(S("oT_ready"), n * TB + ct)
                        for u in range(2):
                            ins = mm(bank[2][u * DH:(u + 1) * DH, 0:2 * P], vt[:, m], pT[j % 4][:, u * 2 * P:(u + 1) * 2 * P],
                                     start=(m == 0), stop=(m == ct))
                        if m == ct:
                            ins.then_inc(S("o2_psum"), 1)

                    weighed = []
                    for score_, blocks, complete, project, add in rounds():
                        if score_:
                            score(*score_)
                        for block_ in blocks:
                            weigh(*block_)
                            weighed.append(block_)
                            if len(weighed) > 2:
                                values(*weighed.pop(0))
                        if complete is not None:
                            while weighed:
                                values(*weighed.pop(0))
                        if project is not None:
                            pe.wait_ge(S("oT_ready"), n * TB + project + 1)
                            pe.wait_ge(S("acc_done"), n * TB + project)
                            for j in range(2):
                                ins = mm(bank[3][:, 0:D], oT[:, j], wo2[:, bass.ds(g, 1), j].rearrange("p o d -> p (o d)"), start=(j == 0), stop=(j == 1))
                            ins.then_inc(S("proj2"), 1)

            pe.wait_ge(S("acc_done"), BATCH * NKV * TB)
            with pe.Fori(0, NT // 2) as i2:
                for q in range(2):
                    i = i2 * 2 + q
                    pe.wait_ge(S("tT_ready"), i2 * 2)
                    pe.wait_ge(S("t_ready"), i + 1)
                    for k in range(KB):
                        ins = nc.tensor.transpose(bank[q][:, k * P:(k + 1) * P], xn2[q][:, k * P:(k + 1) * P], ident[:])
                    ins.then_inc(S("tT_psum"), 1)
                    pe.wait_ge(S("tT_ready"), i + 1)
                    for k in range(KB):
                        ins = mm(bank[2][:, bass.ds(i * E, E)], xnT2[q][:, k], gate[:, k], start=(k == 0), stop=(k == KB - 1))
                    ins.then_inc(S("logits_psum"), 1)
            pe.wait_ge(S("router_steps"), ROUTED)
            mm(bank[0][:, 0:E * NT], tri[:], picked[:].rearrange("p e t -> p (e t)"), start=True, stop=True)
            mm(bank[1][:, 0:E * NT], ones[:], picked[:].rearrange("p e t -> p (e t)"), start=True, stop=True).then_inc(S("ranks_psum"), 1)

            def turn_slot(u, n, loads):
                pe.wait_ge(S("sT_ready"), n)
                pe.wait_ge(S(f"xs_loaded{u}"), loads)
                for k in range(KB):
                    ins = nc.tensor.transpose(bank[3][:, k * P:(k + 1) * P], xs_sb[u][:, k * P:(k + 1) * P], ident[:])
                ins.then_inc(S("sT_psum"), 1)

            turn_slot(0, 0, 16)
            with pe.Fori(0, NS // UR) as it:
                for u in range(UR):
                    slot = it * UR + u
                    pe.wait_ge(S("sT_ready"), slot + 1)
                    pe.wait_ge(S("gated_ready"), slot * 2)
                    for half in range(2):
                        for at, w, name in ((0, "w1", "up_psum"), (2, "w3", "gate_psum")):
                            if half == 0:
                                pe.wait_ge(S(f"{w}_loaded{u}"), 16 * it + 16)
                            w = w1_e[u] if w == "w1" else w3_e[u]
                            for f in range(4):
                                for k in range(KB):
                                    ins = mm(wide[:, at + half, f * P:(f + 1) * P], w[:, k, (half * 4 + f) * P:(half * 4 + f + 1) * P], sT[u][:, k],
                                             start=(k == 0), stop=(k == KB - 1))
                            ins.then_inc(S(name), 1)
                    turn_slot((u + 1) % UR, slot + 1, 16 * it + (16 if u < UR - 1 else 32))
                    pe.wait_ge(S(f"w2_loaded{u}"), 16 * it + 16)
                    pe.wait_ge(S(f"y_ready{u}"), it)
                    for f in range(FB):
                        if f % 4 == 0:
                            pe.wait_ge(S("gated_ready"), slot * 2 + f // 4 + 1)
                        ins = mm(bank[u][:, 0:D], gated[:, f], w2_e[u][:, f], start=(f == 0), stop=(f == FB - 1))
                    ins.then_inc(S(f"slot_done{u}"), 1)


_INS = ["L0_attn_x", "L0_attn_wq", "L0_attn_wk", "L0_attn_wv", "L0_attn_wo", "L0_attn_fq1_w", "L0_attn_fq1_b", "L0_attn_fq2_w",
        "L0_attn_fq2_b", "L0_attn_fk1_w", "L0_attn_fk1_b", "L0_attn_fk2_w", "L0_attn_fk2_b", "L0_attn_norm_w", "L0_ffn_ln1_w",
        "L0_ffn_wq", "L0_ffn_wk", "L0_ffn_wv", "L0_ffn_wo", "L0_ffn_ln2_w", "L0_ffn_gate_w", "L0_ffn_w1", "L0_ffn_w2", "L0_ffn_w3"]


def kernel(**inputs):
    import numpy as _np
    import concourse.bacc as _bacc
    from concourse.bass_utils import run_bass_kernel_spmd as _run

    nc = _bacc.Bacc("TRN2", target_bir_lowering=False, num_devices=1)
    arrays, aps = {}, {}
    for name in _INS:
        x = _np.ascontiguousarray(inputs[name])
        arrays[f"in_{name}"] = x
        aps[name] = nc.dram_tensor(f"in_{name}", x.shape, mybir.dt.from_np(x.dtype), kind="ExternalInput").ap()
    out = nc.dram_tensor("out_0", (BATCH, SEQ, D), F32, kind="ExternalOutput").ap()
    build(nc, aps, out)
    r = _run(nc, [arrays], core_ids=[0])
    return r.results[0]["out_0"]
```

```python
from contextlib import ExitStack

import concourse.bass as bass
from concourse import mybir

F32 = mybir.dt.float32
F32R = mybir.dt.float32r
BF16 = mybir.dt.bfloat16
U32 = mybir.dt.uint32
ALU = mybir.AluOpType
ACT = mybir.ActivationFunctionType
AX = mybir.AxisListType

P = 128
D = 256
KB = D // P
BATCH, SEQ = 2, 1024
NT = BATCH * SEQ // P
TB = SEQ // P
DK = 16
HB = P // DK
NH, NKV, DH = 32, 8, 64
G = NH // NKV
E, F = 8, 1024
FB = F // P
TOPK = 2
NS = TOPK * NT + E - 1
UR = 3
assert NS % UR == 0
RUN = NS // UR
HALF = SEQ // 2
PAIRS = TB * (TB + 1) // 2
EPS = 1e-5
MASKED = -1e30
NCONST = 26
ROUTED = 13


LAG = 2


def rounds():
    order, waiting = [], []
    for ct in range(TB + 2):
        for h in range(G):
            tile, part = (ct - 1, h - 1) if h else (ct - 2, G - 1)
            live = 0 <= tile < TB
            turned = [(tile, m) for m in range((tile + 1) * part // G, (tile + 1) * (part + 1) // G)] if live else []
            weighed = []
            for block in turned:
                waiting.append(block)
                if len(waiting) > LAG:
                    weighed.append((block, waiting.pop(0)))
            if part == G - 1:
                weighed += [(None, block) for block in waiting]
                waiting = []
            done = [t for _, (t, m) in weighed if m == t]
            order.append(((ct, h) if ct < TB else None, turned, weighed, done))
    complete = [x[3] for x in order]
    return [(*x, late, later) for x, late, later in zip(order, [[]] + complete, [[], []] + complete)]


SECOND_HALF = {1: 0, 4: 1, 7: 2}
NEXT_FIRST_HALF = {G * TB + 1: 0, G * TB + 2: 1, G * TB + 3: 2}
VALUES = 5
PROJECTION_BANKS = [[0, 1, 3], [1, 3, 1]]


def evacuates(j):
    return "vector" if j % 4 == 3 and j >= 2 * PAIRS // 3 else "scalar"


def pair(ct, m):
    return ct * (ct + 1) // 2 + m


def build(nc, a, out):
    ctx = ExitStack()
    with ctx:
        def sb(name, shape, dt=F32):
            return ctx.enter_context(nc.sbuf_tensor(name, shape, dt))

        def wait_alone(engine, sem, value):
            value = engine.to_reg(value)
            engine.wait_ge(S("constants_ready"), NCONST)
            engine.wait_ge(sem, value)

        def turned_bank(t, k):
            return wide[:, 2 * t + k, :] if t < 2 else bank[2 * (t - 2) + k][:]

        def x_pairs(x, s):
            return x[:].rearrange("p (b t) d -> p b t d", b=BATCH)[:, :, bass.ds(s, 1)].rearrange("p b o d -> p b (o d)")

        def x_part(x, part):
            return x[:].rearrange("p (b t) -> p b t", b=BATCH)[:, :, 1:TB] if part else x[:].rearrange("p (b t) -> p b t", b=BATCH)[:, :, 0:1]

        sems = {}

        def S(name):
            if name not in sems:
                sems[name] = ctx.enter_context(nc.semaphore(name))
            return sems[name]

        bank = [ctx.enter_context(nc.psum_tensor(f"bank{i}", [P, 512], F32)) for i in range(4)]
        wide = ctx.enter_context(nc.psum_tensor("wide", [P, 4, 512], F32))

        x_all = sb("x_all", [P, NT, D])
        acc = sb("acc", [P, NT, D])
        rT_all = sb("rT_all", [P, KB, NT * P])
        wo2 = sb("wo2", [P, NKV, 2, D])
        ident = sb("ident", [P, P])
        identb = sb("identb", [P, P], BF16)
        tri = sb("tri", [P, P])
        above = sb("above", [P, P], BF16)
        headmask = sb("headmask", [P, HB])
        experts = sb("experts", [P, E])
        neghalf = sb("neghalf", [P, 1])
        arena = sb("arena", [P, UR * 3 * KB * F])

        def part(at, n, pattern, **dims):
            return arena[:, at:at + n].rearrange(pattern, **dims)

        w_size = KB * F
        w1_e = [part((3 * u) * w_size, w_size, "p (k f) -> p k f", k=KB) for u in range(UR)]
        w3_e = [part((3 * u + 1) * w_size, w_size, "p (k f) -> p k f", k=KB) for u in range(UR)]
        w2_e = [part((3 * u + 2) * w_size, w_size, "p (f d) -> p f d", f=FB) for u in range(UR)]
        wnat = part(0, 4 * KB * D, "p (w k d) -> p w k d", w=4, k=KB)
        small = sb("small", [DK, 4 * DK + 5])
        rep = sb("rep", [DK, HB, DK])
        bd = sb("bd", [P, HB, DK])
        fdiagT = sb("fdiagT", [P, 4, HB, DK])
        wfeat = part(4 * KB * D, 4 * KB * D, "p (w k d) -> p w k d", w=4, k=KB)
        wvT = part(8 * KB * D, KB * D, "p (k d) -> p k d", k=KB)
        woT = part(9 * KB * D, KB * D, "p (k d) -> p k d", k=KB)
        smallr = sb("smallr", [P, 5])
        fbias = smallr[:, 0:4]
        normw = smallr[:, 4:5]
        fbias_q = sb("fbias_q", [P, 1])
        ln1 = sb("ln1", [P, KB])
        ln2 = sb("ln2", [P, KB])
        gate = sb("gate", [P, KB, E])
        at = 10 * KB * D
        n = KB * BATCH * HB * P
        qx = part(at, n, "p (k b h c) -> p k b h c", k=KB, b=BATCH, h=HB)
        sm = part(at + n, n, "p (k b h c) -> p k b h c", k=KB, b=BATCH, h=HB)
        vp = part(at + 2 * n, BATCH * 2 * D, "p (b j c e) -> p b j c e", b=BATCH, c=4, e=DK)
        vpad = part(at + 2 * n, BATCH * 2 * D, "p (b k j r e) -> p b k j r e", b=BATCH, k=KB, r=2, e=2 * DK)

        spare = wo2[:].rearrange("p g j d -> p (g j d)")

        def pair_tile(i):
            n = KB * BATCH * P
            return spare[:, i * n:(i + 1) * n].rearrange("p (k b c) -> p k b c", k=KB, b=BATCH)

        xn = sb("xn", [P, BATCH, D])
        xnT = sb("xnT", [P, KB, BATCH, P])
        q1s = pair_tile(0)
        k1s = pair_tile(1)
        qT = pair_tile(2)
        kT = pair_tile(3)
        ktok = pair_tile(4)
        kvt = pair_tile(7)
        state = sb("state", [P, KB, BATCH, P])
        osq = pair_tile(5)
        orstd = sb("orstd", [P, KB * BATCH * P])
        oms = sb("oms", [P, KB * BATCH * P])
        onT = pair_tile(6)
        st6 = sb("st6", [P, BATCH, 6])
        mv = sb("mv", [P, BATCH, 2])
        ve = sb("ve", [P, BATCH])
        rstd = sb("rstd", [P, BATCH])
        aon = sb("aon", [P, BATCH, D])
        rn = sb("rn", [P, BATCH, D])
        ysum = sb("ysum", [P, BATCH])
        junk = sb("junk", [P, BATCH, D])
        wq_g = sb("wq_g", [P, KB, G * DH])
        wkv_g = sb("wkv_g", [P, KB, 2 * DH])
        khi = sb("khi", [P, SEQ], F32R)
        qhl = sb("qhl", [P, G, SEQ], F32R)
        klo = sb("klo", [P, SEQ], F32R)
        vT = sb("vT", [DH, SEQ])
        vt = sb("vt", [P, TB, DH])
        probs = [part(i * G * SEQ, G * SEQ, "p (h m) -> p h m", h=G) for i in range(3)]
        nmax = sb("nmax", [P, 3, G])
        rsum = sb("rsum", [P, 3, G])
        rinv = sb("rinv", [P, 3, G])
        pT = [part(3 * G * SEQ + i * G * P, G * P, "p (o c) -> p (o c)", o=1) for i in range(4)]
        oT = sb("oT", [P, 2, P])
        hss = sb("hss", [P, NT])
        hve = sb("hve", [P, NT])
        hrstd = sb("hrstd", [P, NT])
        hmean = sb("hmean", [P, NT, 2])
        stf = sb("stf", [P, NT, 6])
        hT = part(0, KB * NT * P, "p (k n) -> p k n", k=KB)
        squares = part(KB * NT * P, NT * D, "p (t d) -> p t d", t=NT)
        t_all = rT_all[:].rearrange("p k n -> p (k n)").rearrange("p (t c) -> p t c", t=NT)
        glog = sb("glog", [P, NT, E])
        gmax = sb("gmax", [P, NT])
        gsum = sb("gsum", [P, NT])
        top = sb("top", [P, NT, 8])
        topi = sb("topi", [P, NT, 8], U32)
        topf = sb("topf", [P, NT, TOPK])
        topw = sb("topw", [P, NT, TOPK])
        pick = sb("pick", [P, TOPK, E, NT])
        picked = sb("picked", [P, E, NT])
        upto = sb("upto", [P, E, NT])
        place = sb("place", [P, E, NT])
        full = sb("full", [P, E, NT])
        nslots = sb("nslots", [P, E])
        endslot = sb("endslot", [P, E])
        startrow = sb("startrow", [P, E])
        prod = sb("prod", [P, TOPK, E, NT])
        row = sb("row", [P, TOPK, NT])
        rowi = sb("rowi", [P, TOPK, NT], U32)
        passed = sb("passed", [1, NS, E])
        slote = sb("slote", [1, NS])
        slotm = sb("slotm", [1, NS])
        slotei = sb("slotei", [1, NS], mybir.dt.int32)
        change = sb("change", [1, NS])
        starts = sb("starts", [1, NS])
        loads = sb("loads", [1, NS])
        freshi = sb("freshi", [1, NS], mybir.dt.int32)
        hundreds = sb("hundreds", [P, NT])
        slotno = sb("slotno", [1, NS])
        restart = sb("restart", [P, E, NT])
        ones = sb("ones", [P, P])
        eps = sb("eps", [P, 1])
        zeros = sb("zeros", [P, D])
        relu = [spare[:, i * 4 * P:(i + 1) * 4 * P] for i in range(2)]
        gated = spare[:, 8 * P:(8 + FB) * P].rearrange("p (f c) -> p f c", f=FB)
        xs_sb = [spare[:, (16 + KB * u) * P:(16 + KB * (u + 1)) * P] for u in range(UR)]
        sT = [spare[:, (24 + KB * u) * P:(24 + KB * (u + 1)) * P].rearrange("p (k c) -> p k c", k=KB) for u in range(UR)]
        y_sb = [sb(f"y_sb{u}", [P, D]) for u in range(UR)]
        yg = part(0, NT * TOPK * D, "p (t k d) -> p t k d", t=NT, k=TOPK)
        xs = nc.dram_tensor("xs", (NS * P, D), F32, kind="Internal").ap()
        ys = nc.dram_tensor("ys", (NS * P, D), F32, kind="Internal").ap()

        block = ctx.enter_context(nc.Block())

        @block.sync
        def _(sp):
            for n, w in enumerate(("fq1", "fq2", "fk1", "fk2")):
                sp.dma_start(small[:, n * DK:(n + 1) * DK], a[f"L0_attn_{w}_w"].rearrange("e d -> d e"), allow_slow_non_contiguous=True).then_inc(S("small_loaded"), 16)
            for n, w in enumerate(("fq1_b", "fq2_b", "fk1_b", "fk2_b", "norm_w")):
                sp.dma_start(small[:, 4 * DK + n:4 * DK + n + 1], a[f"L0_attn_{w}"].rearrange("(e o) -> e o", o=1)).then_inc(S("small_loaded"), 16)
            for n, w in enumerate(("wq", "wk", "wv", "wo")):
                sp.dma_start(wnat[:, n], a[f"L0_attn_{w}"].rearrange("(k p) d -> p k d", p=P)).then_inc(S("wnat_loaded"), 16)
            for t, w in ((ln1, "ln1_w"), (ln2, "ln2_w")):
                for k in range(KB):
                    sp.dma_start(t[:, k:k + 1], a[f"L0_ffn_{w}"][k * P:(k + 1) * P].rearrange("(e o) -> e o", o=1)).then_inc(S("ln_loaded"), 16)
            sp.dma_start(gate[:], a["L0_ffn_gate_w"].rearrange("(k p) e -> p k e", p=P)).then_inc(S("ln_loaded"), 16)
            wo_v = a["L0_ffn_wo"].rearrange("(g u j d) n -> u d g j n", g=NKV, u=2, j=2)
            wq_v = a["L0_ffn_wq"].rearrange("(k p) n -> p k n", p=P)
            wk_v = a["L0_ffn_wk"].rearrange("(k p) n -> p k n", p=P)
            wv_v = a["L0_ffn_wv"].rearrange("(k p) n -> p k n", p=P)

            def load_group(g):
                sp.dma_start(wq_g[:], wq_v[:, :, bass.ds(g * (G * DH), G * DH)]).then_inc(S("wq_loaded"), 16)
                sp.dma_start(wkv_g[:, :, 0:DH], wk_v[:, :, bass.ds(g * DH, DH)]).then_inc(S("wk_loaded"), 16)
                sp.dma_start(wkv_g[:, :, DH:2 * DH], wv_v[:, :, bass.ds(g * DH, DH)]).then_inc(S("wv_loaded"), 16)

            load_group(0)
            sp.wait_ge(S("rT_ready"), TB)
            for u in range(2):
                for g in range(NKV):
                    sp.dma_start(wo2[u * DH:(u + 1) * DH, g], wo_v[u][:, g]).then_inc(S("wo2_loaded"), 16)
            with sp.Fori(1, NKV) as g:
                sp.wait_ge(S("projected"), g * (6 * BATCH))
                load_group(g)
            sp.wait_ge(S("projected"), NKV * 6 * BATCH)
            load_group(NKV - 1)
            w1_v = a["L0_ffn_w1"].rearrange("e (k p) f -> p e k f", p=P)
            w3_v = a["L0_ffn_w3"].rearrange("e (k p) f -> p e k f", p=P)
            w2_v = a["L0_ffn_w2"].rearrange("e (f p) d -> p e f d", p=P)
            xs_v = xs.rearrange("(s p) d -> p s d", p=P)
            sp.wait_ge(S("slots_known"), 1)
            with sp.Fori(0, NS // UR) as it:
                for u in range(UR):
                    sp.wait_ge(S(f"slot_done{u}"), it)
                    slot = it + u * RUN
                    e = sp.value_load(slotei[0:1, bass.ds(slot, 1)], min_val=0, max_val=E - 1)
                    fresh = sp.value_load(freshi[0:1, bass.ds(slot, 1)], min_val=0, max_val=1)
                    sp.dma_start(w1_e[u], w1_v[:, bass.ds(e, 1)].rearrange("p o k f -> p (o k) f"), cond=fresh != 0).then_inc(S(f"w1_loaded{u}"), 16)
                    sp.dma_start(w3_e[u], w3_v[:, bass.ds(e, 1)].rearrange("p o k f -> p (o k) f"), cond=fresh != 0).then_inc(S(f"w3_loaded{u}"), 16)
                    sp.dma_start(w2_e[u], w2_v[:, bass.ds(e, 1)].rearrange("p o f d -> p (o f) d"), cond=fresh != 0).then_inc(S(f"w2_loaded{u}"), 16)
                    sp.wait_ge(S("xs_scattered"), 16 * TOPK * NT)
                    sp.dma_start(xs_sb[u], xs_v[:, bass.ds(slot, 1)].rearrange("p o d -> p (o d)")).then_inc(S(f"xs_loaded{u}"), 16)
            sp.wait_ge(S("slot_done0"), NS // UR)
            sp.dma_start(xs_sb[0], xs_v[:, NS - 1]).then_inc(S("xs_loaded0"), 16)
            out_v = out.rearrange("b (t p) d -> p (b t) d", p=P)
            for i in range(NT):
                sp.wait_ge(S("out_ready"), i + 1)
                sp.dma_start(out_v[:, i:i + 1], x_all[:, i:i + 1]).then_inc(S("stored"), 16)
            sp.wait_ge(S("stored"), 16 * NT)

        @block.gpsimd
        def _(gp):
            nc.gpsimd.memset(ident[:], 0.0).then_inc(S("constants_ready"), 1)
            nc.gpsimd.memset(tri[:], 1.0).then_inc(S("constants_ready"), 1)
            nc.gpsimd.memset(above[:], 0.0).then_inc(S("constants_ready"), 1)
            nc.gpsimd.memset(headmask[:], 1.0).then_inc(S("constants_ready"), 1)
            nc.gpsimd.memset(eps[:], EPS).then_inc(S("constants_ready"), 1)
            nc.gpsimd.memset(neghalf[:], -0.5).then_inc(S("constants_ready"), 1)
            nc.gpsimd.iota(experts[:], [[1, E]], base=0, channel_multiplier=0,
                           allow_small_or_imprecise_dtypes=True).then_inc(S("constants_ready"), 1)
            nc.gpsimd.iota(hundreds[:], [[P, NT]], base=0, channel_multiplier=0,
                           allow_small_or_imprecise_dtypes=True).then_inc(S("constants_ready"), 1)
            nc.gpsimd.iota(slotno[:], [[1, NS]], base=0, channel_multiplier=0,
                           allow_small_or_imprecise_dtypes=True).then_inc(S("constants_ready"), 1)
            nc.gpsimd.memset(ones[:], 1.0).then_inc(S("constants_ready"), 1)
            nc.gpsimd.memset(zeros[:], 0.0).then_inc(S("constants_ready"), 1)
            nc.gpsimd.memset(restart[:], 1.0).then_inc(S("constants_ready"), 1)
            nc.gpsimd.memset(change[:], 0.0).then_inc(S("constants_ready"), 1)
            nc.gpsimd.memset(starts[:], 0.0).then_inc(S("constants_ready"), 1)
            gp.wait_ge(S("constants_ready"), 14)
            nc.gpsimd.affine_select(out=ident[:], in_=ident[:], compare_op=ALU.not_equal, fill=1.0, base=0,
                                    pattern=[[-1, P]], channel_multiplier=1).then_inc(S("constants_ready"), 1)
            nc.gpsimd.affine_select(out=tri[:], in_=tri[:], compare_op=ALU.is_ge, fill=0.0, base=0,
                                    pattern=[[1, P]], channel_multiplier=-1).then_inc(S("constants_ready"), 1)
            nc.gpsimd.affine_select(out=above[:], in_=above[:], compare_op=ALU.is_ge, fill=MASKED, base=0,
                                    pattern=[[-1, P]], channel_multiplier=1).then_inc(S("constants_ready"), 1)
            nc.gpsimd.affine_select(out=headmask[:], in_=headmask[:], compare_op=ALU.is_ge, fill=0.0, base=0,
                                    pattern=[[-DK, HB]], channel_multiplier=1).then_inc(S("constants_ready"), 1)
            nc.gpsimd.memset(restart[:, :, 0:1], 0.0).then_inc(S("constants_ready"), 1)
            nc.gpsimd.memset(starts[:, 0:NS:RUN], 1.0).then_inc(S("constants_ready"), 1)
            gp.wait_ge(S("constants_ready"), 20)
            nc.gpsimd.affine_select(out=headmask[:], in_=headmask[:], compare_op=ALU.is_ge, fill=0.0, base=DK - 1,
                                    pattern=[[DK, HB]], channel_multiplier=-1).then_inc(S("constants_ready"), 1)
            nc.gpsimd.tensor_copy(identb[:], ident[:]).then_inc(S("constants_ready"), 1)
            nc.gpsimd.tensor_copy(rep[:], ident[0:DK, 0:DK].rearrange("p (o e) -> p o e", o=1).to_broadcast([DK, HB, DK])).then_inc(S("constants_ready"), 1)
            nc.gpsimd.memset(vp[:], 0.0).then_inc(S("constants_ready"), 1)
            nc.gpsimd.memset(state[:], 0.0).then_inc(S("constants_ready"), 1)
            gp.wait_ge(S("constants_ready"), NCONST - 1)
            nc.gpsimd.tensor_scalar(bd[:], headmask[:].rearrange("p (h o) -> p h o", o=1).to_broadcast([P, HB, DK]), 1.0 / DK, None, ALU.mult).then_inc(S("constants_ready"), 1)

            def power(i, n, dst, src, asked, given):
                gp.wait_ge(S(asked), i + 1)
                nc.gpsimd.tensor_tensor(dst, src, neghalf[:].to_broadcast([P, n]), ALU.pow).then_inc(S(given), 1)
            def x_power(part):
                gp.wait_ge(S("ve_x"), part + 1)
                dst = x_part(hrstd, part)
                nc.gpsimd.tensor_tensor(dst, x_part(hve, part), neghalf[:].rearrange("p (o t) -> p o t", o=1).to_broadcast(dst.shape), ALU.pow).then_inc(S("rstd_x"), 1)

            x_power(0)

            def pair_step(s, front, back):
                if front:
                    gp.wait_ge(S("qT_ready"), s + 1)
                    if front and back:
                        gp.wait_ge(S("scores1"), 4 * s)
                    for b in range(BATCH):
                        nc.gpsimd.tensor_tensor(qx[:, 0, b], qT[:, 0, b:b + 1, :].to_broadcast([P, HB, P]),
                                                headmask[:].rearrange("p (h o) -> p h o", o=1).to_broadcast([P, HB, P]),
                                                ALU.mult).then_inc(S("qx0_ready"), 1)
                if back:
                    for name in ("ao", "x1", "y"):
                        power(s - 1, BATCH, rstd[:], ve[:], "ve_" + name, "rstd_" + name)

            pair_step(0, True, False)
            x_power(1)
            with gp.Fori(1, TB) as s:
                pair_step(s, True, True)
            pair_step(TB, False, True)
            gp.dma_start(xs.rearrange("(s p) d -> p s d", p=P), zeros[:].rearrange("p (o d) -> p o d", o=1).to_broadcast([P, NS, D])).then_inc(S("xs_zeroed"), 16)

            def double(n, half):
                cols = slice(half * HALF, (half + 1) * HALF)
                wait_alone(gp, S("khi_ready"), n * 2 + half + 1)
                if not (type(n) is int and n == half == 0):
                    wait_alone(gp, S("k_doubled"), n * 2 + half)
                nc.gpsimd.tensor_copy(khi[DH:P, cols], khi[0:DH, cols]).then_inc(S("khi_doubled"), 1)
                wait_alone(gp, S("khi_doubled"), n * 2 + half + 1)
                wait_alone(gp, S("klo_ready"), n * 2 + half + 1)
                nc.gpsimd.tensor_copy(klo[DH:P, cols], klo[0:DH, cols]).then_inc(S("k_doubled"), 1)

            double(0, 0)
            with gp.Fori(0, NKV) as g:
                for b in range(BATCH):
                    double(g * BATCH + b, 1)
                    double(g * BATCH + b + 1, 0)
            gp.wait_ge(S("k_doubled"), 2 * NKV * BATCH + 1)
            power(0, NT, hrstd[:], hve[:], "ve_h", "rstd_h")
            gp.wait_ge(S("t_ready"), 1)
            gp.wait_ge(S("rows_known"), 1)
            gp.wait_ge(S("xs_zeroed"), 16)
            for t in range(NT):
                for k in range(TOPK):
                    nc.gpsimd.indirect_dma_start(out=xs, out_offset=bass.IndirectOffsetOnAxis(ap=rowi[:, k, t:t + 1], axis=0),
                                                 in_=t_all[:, t], in_offset=None).then_inc(S("xs_scattered"), 16)
            ys_v = ys.rearrange("(s p) d -> p s d", p=P)
            with gp.Fori(0, NS // UR) as it:
                for u in range(UR):
                    gp.wait_ge(S(f"y_ready{u}"), it + 1)
                    gp.dma_start(ys_v[:, bass.ds(it + u * RUN, 1)].rearrange("p o d -> p (o d)"), y_sb[u][:]).then_inc(S(f"ys_stored{u}"), 16)
            for u in range(UR):
                gp.wait_ge(S(f"ys_stored{u}"), 16 * (NS // UR))
            for t in range(NT):
                for k in range(TOPK):
                    nc.gpsimd.indirect_dma_start(out=yg[:, t, k], out_offset=None, in_=ys,
                                                 in_offset=bass.IndirectOffsetOnAxis(ap=rowi[:, k, t:t + 1], axis=0)).then_inc(S(f"gathered{t // 4}"), 16)

        @block.scalar
        def _(act):
            act.dma_start(x_all[:], a["L0_attn_x"].rearrange("b (t p) d -> p (b t) d", p=P)).then_inc(S("x_loaded"), 16)
            act.wait_ge(S("small_psum"), 1)
            nc.scalar.copy(smallr[:], bank[3][:, 4 * DK:4 * DK + 5]).then_inc(S("smallr_ready"), 1)
            act.wait_ge(S("smallr_ready"), 1)
            nc.scalar.activation(fbias_q[:], smallr[:, 0:1], ACT.Copy, scale=DK ** -0.5).then_inc(S("fbias_q_ready"), 1)
            act.wait_ge(S("fbias_q_ready"), 1)
            act.wait_ge(S("wT_psum"), 1)
            nc.scalar.copy(wvT, bank[2][:].rearrange("p (k d) -> p k d", k=KB)).then_inc(S("wT_ready"), 1)
            act.wait_ge(S("wT_psum"), 2)
            nc.scalar.activation(woT, bank[3][:].rearrange("p (k d) -> p k d", k=KB), ACT.Copy, scale=normw).then_inc(S("wT_ready"), 1)
            for n in range(4):
                act.wait_ge(S("wfeat_psum"), n + 1)
                nc.scalar.copy(wfeat[:, n], wide[:, n, :].rearrange("p (k d) -> p k d", k=KB)).then_inc(S("wfeat_ready"), 1)

            def whole(x):
                return x.rearrange("p k b c -> p (k b c)")

            def pair_step(s, front, back):
                if front:
                    act.wait_ge(S("xnT_psum"), s + 1)
                    if back:
                        act.wait_ge(S("v_psum"), s)
                    nc.scalar.copy(whole(xnT[:]), bank[3][:]).then_inc(S("xnT_ready"), 1)
                if back:
                    act.wait_ge(S("o_psum"), s)
                    if front:
                        act.wait_ge(S("oms_psum"), s - 1)
                    nc.scalar.activation(whole(osq), bank[2][:], ACT.Square).then_inc(S("osq_ready"), 1)
                if front:
                    act.wait_ge(S("q1_psum"), s + 1)
                    if back:
                        act.wait_ge(S("qT_ready"), s)
                    nc.scalar.activation(whole(q1s), bank[0][:], ACT.Identity, bias=fbias_q[:, 0:1], scale=DK ** -0.5).then_inc(S("q1_ready"), 1)
                if back:
                    act.wait_ge(S("oms_psum"), s)
                    if front:
                        act.wait_ge(S("orstd_ready"), s - 1)
                    nc.scalar.activation(oms[:], bank[3][:], ACT.Sqrt, bias=eps[:, 0:1]).then_inc(S("oms_ready"), 1)
                if front:
                    act.wait_ge(S("k1_psum"), s + 1)
                    if back:
                        act.wait_ge(S("kT_ready"), s)
                    nc.scalar.activation(whole(k1s), bank[0][:], ACT.Identity, bias=fbias[:, 2:3]).then_inc(S("k1_ready"), 1)
                    act.wait_ge(S("qT_ready"), s + 1)
                    if back:
                        act.wait_ge(S("scores1"), 4 * s)
                    for h in range(HB):
                        ins = nc.scalar.activation(qx[:, 1, :, h], qT[:, 1], ACT.Copy, scale=headmask[:, h:h + 1])
                    ins.then_inc(S("qx1_ready"), 1)
                    act.wait_ge(S("v_psum"), s + 1)
                    if back:
                        act.wait_ge(S("kv_psum"), s)
                    for b in range(BATCH):
                        ins = nc.scalar.copy(vp[:, b, :, 0:4:3], bank[3][:, b * D:(b + 1) * D].rearrange("p (j r e) -> p j r e", r=2, e=DK))
                    ins.then_inc(S("v_ready"), 1)
                    act.wait_ge(S("ktok_psum"), s + 1)
                    nc.scalar.copy(whole(ktok), bank[1][:]).then_inc(S("ktok_ready"), 1)
                if back:
                    tile = x_pairs(acc, s - 1)
                    act.wait_ge(S("y_ready"), s)
                    if front:
                        act.wait_ge(S("yss_ready"), s - 1)
                    for b in range(BATCH):
                        ins = nc.scalar.activation(junk[:, b], tile[:, b], ACT.Square, accum_out=ysum[:, b:b + 1])
                    ins.then_inc(S("yss_ready"), 1)
                    wait_alone(act, S("rstd_y"), s)
                    if front:
                        act.wait_ge(S("rT_psum"), s - 1)
                    for b in range(BATCH):
                        ins = nc.scalar.activation(rn[:, b], tile[:, b], ACT.Copy, scale=rstd[:, b:b + 1])
                    ins.then_inc(S("r_ready"), 1)
                    act.wait_ge(S("rT_psum"), s)
                    for k in range(KB):
                        ins = nc.scalar.activation(rT_all[:, k].rearrange("p (b t c) -> p b t c", b=BATCH, t=TB)[:, :, bass.ds(s - 1, 1)].rearrange("p b o c -> p b (o c)"),
                                                   bank[1][:, k * BATCH * P:(k + 1) * BATCH * P].rearrange("p (b c) -> p b c", b=BATCH), ACT.Copy, scale=ln1[:, k:k + 1])
                    ins.then_inc(S("rT_ready"), 1)

            act.wait_ge(S("constants_ready"), NCONST)
            nc.scalar.activation(junk[:, 0, 0:1], eps[:], ACT.Sqrt).then_inc(S("sqrt_loaded"), 1)
            act.wait_ge(S("sqrt_loaded"), 1)
            act.wait_ge(S("ln_loaded"), 16 * (2 * KB + 1))
            pair_step(0, True, False)
            with act.Fori(1, TB) as s:
                pair_step(s, True, True)
            pair_step(TB, False, True)
            def evacuate(n, half, i):
                cols = slice(half * HALF, (half + 1) * HALF)
                src = wide[:, PROJECTION_BANKS[half][i], :]
                act.wait_ge(S("projected"), n * 6 + half * 3 + i + 1)
                if i == 0:
                    nc.scalar.copy(khi[0:DH, cols], src[0:DH]).then_inc(S("khi_ready"), 1)
                    nc.scalar.copy(vT[:, cols], src[DH:P]).then_inc(S("vT_ready"), 1)
                else:
                    for u in range(2):
                        ins = nc.scalar.activation(qhl[0:DH, 2 * (i - 1) + u, cols], src[u * DH:(u + 1) * DH], ACT.Copy, scale=DH ** -0.5)
                    ins.then_inc(S("qhi_ready"), 1)

            nc.scalar.activation(junk[:, 0, 0:1], eps[:], ACT.Exp).then_inc(S("exp_loaded"), 1)
            act.wait_ge(S("exp_loaded"), 1)
            for i in range(3):
                evacuate(0, 0, i)
            with act.Fori(0, NKV) as g:
                for b in range(BATCH):
                    n = g * BATCH + b
                    for r, (score, turned, weighed, complete, project, add) in enumerate(rounds()):
                        if r - 1 in NEXT_FIRST_HALF:
                            evacuate(n + 1, 0, NEXT_FIRST_HALF[r - 1])
                        for ct, m in turned:
                            j = pair(ct, m)
                            if evacuates(j) == "scalar":
                                act.wait_ge(S("pT_psum"), n * PAIRS + j + 1)
                                nc.scalar.copy(pT[j % 4], bank[j % 2][:]).then_inc(S("pT_odd" if j % 2 else "pT_even"), 1)
                        if score:
                            ct, h = score
                            w = (ct + 1) * P
                            act.wait_ge(S("nmax_ready"), n * (TB * G) + ct * G + h + 1)
                            nc.scalar.activation(probs[ct % 3][:, h, 0:w],
                                                 wide[:, 2 * (h % 2):2 * (h % 2) + 2, :].rearrange("p a b -> p (a b)")[:, 0:w],
                                                 ACT.Exp, bias=nmax[:, ct % 3, h:h + 1],
                                                 accum_out=rsum[:, ct % 3, h:h + 1]).then_inc(S("exp_done"), 1)
                        if r - 1 in SECOND_HALF:
                            evacuate(n, 1, SECOND_HALF[r - 1])
                        for ct in complete:
                            act.wait_ge(S("o2_psum"), n * TB + ct + 1)
                            nc.scalar.copy(oT[:], bank[2][:, 0:2 * P].rearrange("p (j c) -> p j c", j=2)).then_inc(S("oT_ready"), 1)
            act.wait_ge(S("acc_done"), BATCH * NKV * TB)
            for t in range(NT // 4):
                act.wait_ge(S("hT_psum"), 2 * t + 1)
                nc.scalar.copy(hT[:, 0, t * 4 * P:(t + 1) * 4 * P], turned_bank(t, 0)).then_inc(S("hT0_ready"), 1)
            for i in range(NT):
                ins = nc.scalar.activation(squares[:, i], acc[:, i], ACT.Square, accum_out=hss[:, i:i + 1])
            ins.then_inc(S("hss_ready"), 1)
            act.wait_ge(S("glog_ready"), 1)
            nc.scalar.activation(glog[:], glog[:], ACT.Exp).then_inc(S("gexp_ready"), 1)
            for i in range(NT):
                ins = nc.scalar.activation(t_all[:, i], acc[:, i], ACT.Copy, scale=hrstd[:, i:i + 1])
            ins.then_inc(S("t_ready"), 1)

            def evacuate_slot(u, n):
                act.wait_ge(S("sT_psum"), n)
                for k in range(KB):
                    ins = nc.scalar.activation(sT[u][:, k], bank[3][:, k * P:(k + 1) * P], ACT.Copy, scale=ln2[:, k:k + 1])
                ins.then_inc(S("sT_ready"), 1)

            evacuate_slot(0, 1)
            with act.Fori(0, NS // UR) as it:
                for u in range(UR):
                    slot = it * UR + u
                    for half in range(2):
                        act.wait_ge(S("up_psum"), slot * 2 + half + 1)
                        act.wait_ge(S("gated_ready"), slot * 2)
                        nc.scalar.activation(relu[half], wide[:, half, :], ACT.Relu).then_inc(S("relu_ready"), 1)
                    evacuate_slot((u + 1) % UR, slot + 2)
                    act.wait_ge(S(f"slot_done{u}"), it + 1)
                    act.wait_ge(S(f"ys_stored{u}"), 16 * it)
                    nc.scalar.copy(y_sb[u][:], bank[u][:, 0:D]).then_inc(S(f"y_ready{u}"), 1)

            for quarter in range(4):
                cols = slice(quarter * (NT // 4), (quarter + 1) * (NT // 4))
                act.wait_ge(S("mean_f"), quarter + 1)
                nc.scalar.activation(hve[:, cols], hmean[:, cols, 1], ACT.Sqrt, bias=eps[:, 0:1]).then_inc(S("std_f"), 1)

        @block.vector
        def _(v):
            v.wait_ge(S("constants_ready"), NCONST)
            v.wait_ge(S("small_psum"), 1)
            v.wait_ge(S("smallr_ready"), 1)
            for n in range(4):
                ins = nc.vector.tensor_tensor(fdiagT[:, n], bank[3][:, n * DK:(n + 1) * DK].rearrange("p (o e) -> p o e", o=1).to_broadcast([P, HB, DK]),
                                              headmask[:].rearrange("p (h o) -> p h o", o=1).to_broadcast([P, HB, DK]), ALU.mult)
            ins.then_inc(S("fdiag_ready"), 1)
            v.wait_ge(S("ln_loaded"), 16 * (2 * KB + 1))
            for k in range(KB):
                ins = nc.vector.tensor_scalar(gate[:, k], gate[:, k], ln2[:, k:k + 1], None, ALU.mult)
            ins.then_inc(S("gate_ready"), 1)
            v.wait_ge(S("x_loaded"), 16)
            def x_statistics(part):
                tiles = [i for i in range(NT) if (i % TB > 0) == part]
                for i in tiles:
                    ins = nc.vector.bn_stats(stf[:, i], x_all[:, i])
                ins.then_inc(S("ve_x_st"), 1)
                v.wait_ge(S("ve_x_st"), part + 1)
                for i in tiles:
                    ins = nc.vector.bn_aggr(hmean[:, i], stf[:, i])
                ins.then_inc(S("ve_x_mv"), 1)
                v.wait_ge(S("ve_x_mv"), part + 1)
                nc.vector.tensor_scalar(x_part(hve, part), x_part(hmean[:, :, 1], part), EPS, None, ALU.add).then_inc(S("ve_x"), 1)

            x_statistics(0)
            v.wait_ge(S("rstd_x"), 1)

            def variance(i, src, name):
                for b in range(BATCH):
                    ins = nc.vector.bn_stats(st6[:, b], src[:, b])
                ins.then_inc(S(f"ve_{name}_st"), 1)
                wait_alone(v, S(f"ve_{name}_st"), i)
                for b in range(BATCH):
                    ins = nc.vector.bn_aggr(mv[:, b], st6[:, b])
                ins.then_inc(S(f"ve_{name}_mv"), 1)
                v.wait_ge(S(f"ve_{name}_mv"), i)
                nc.vector.tensor_scalar(ve[:], mv[:, :, 1], EPS, None, ALU.add).then_inc(S("ve_" + name), 1)

            def pair_step(s, front, back):
                def mask(half):
                    v.wait_ge(S("scores1"), 4 * s + half + 1)
                    nc.vector.tensor_tensor(sm[:, half // 2, half % 2],
                                            wide[:, 2 * (half % 2):2 * (half % 2) + 2].rearrange("p a (h c) -> p (a h) c", c=P),
                                            tri[:].rearrange("p (o c) -> p o c", o=1).to_broadcast([P, HB, P]), ALU.mult).then_inc(S("sm_ready"), 1)

                if front:
                    xt, means, stds = x_pairs(x_all, s), x_pairs(hmean, s), hrstd[:].rearrange("p (b t) -> p b t", b=BATCH)[:, :, bass.ds(s, 1)]
                    if back:
                        v.wait_ge(S("xnT_psum"), s)
                    for b in range(BATCH):
                        ins = nc.vector.tensor_scalar(xn[:, b], xt[:, b], means[:, b, 0:1], stds[:, b], ALU.subtract, ALU.mult)
                    ins.then_inc(S("xn_ready"), 1)
                    if not back:
                        x_statistics(1)
                if back:
                    v.wait_ge(S("o_psum"), s)
                    v.wait_ge(S("kvt_ready"), s)
                    nc.vector.tensor_tensor(state[:], state[:], kvt, ALU.add).then_inc(S("state_ready"), 1)
                halves = orstd[:].rearrange("p (k c) -> p k c", k=KB), oms[:].rearrange("p (k c) -> p k c", k=KB)
                if back:
                    v.wait_ge(S("oms_ready"), s)
                    nc.vector.reciprocal(halves[0][:, 0], halves[1][:, 0])
                if front:
                    v.wait_ge(S("q1_ready"), s + 1)
                    v.wait_ge(S("q2_psum"), s + 1)
                    nc.vector.scalar_tensor_tensor(out=whole(qT), in0=bank[1][:], scalar=fbias[:, 1:2], in1=whole(q1s),
                                                   op0=ALU.add, op1=ALU.mult).then_inc(S("qT_ready"), 1)
                if back:
                    nc.vector.reciprocal(halves[0][:, 1], halves[1][:, 1]).then_inc(S("orstd_ready"), 1)
                    v.wait_ge(S("orstd_ready"), s)
                    nc.vector.tensor_tensor(whole(onT), bank[2][:], orstd[:], ALU.mult).then_inc(S("onT_ready"), 1)
                if front:
                    v.wait_ge(S("k1_ready"), s + 1)
                    v.wait_ge(S("k2_psum"), s + 1)
                    nc.vector.scalar_tensor_tensor(out=whole(kT), in0=bank[1][:], scalar=fbias[:, 3:4], in1=whole(k1s),
                                                   op0=ALU.add, op1=ALU.mult).then_inc(S("kT_ready"), 1)
                if back:
                    xb, yb = x_pairs(x_all, s - 1), x_pairs(acc, s - 1)
                    wait_alone(v, S("ao_psum"), s)
                    ao = bank[0][:].rearrange("p (b d) -> p b d", b=BATCH)
                    variance(s, ao, "ao")
                if back:
                    v.wait_ge(S("rstd_ao"), s)
                    for b in range(BATCH):
                        ins = nc.vector.tensor_scalar(aon[:, b], ao[:, b], mv[:, b, 0:1], rstd[:, b:b + 1], ALU.subtract, ALU.mult)
                    ins.then_inc(S("aon_ready"), 1)
                    v.wait_ge(S("aon_ready"), s)
                    nc.vector.tensor_tensor(xb, xb, aon[:], ALU.add).then_inc(S("x1_ready"), 1)
                    wait_alone(v, S("x1_ready"), s)
                    variance(s, xb, "x1")
                if front:
                    mask(0)
                if back:
                    v.wait_ge(S("rstd_x1"), s)
                    for b in range(BATCH):
                        ins = nc.vector.tensor_scalar(yb[:, b], xb[:, b], mv[:, b, 0:1], rstd[:, b:b + 1], ALU.subtract, ALU.mult)
                    ins.then_inc(S("y_ready"), 1)
                if front:
                    mask(1)
                if back:
                    v.wait_ge(S("yss_ready"), s)
                    nc.vector.tensor_scalar(ve[:], ysum[:], 1.0 / D, EPS, ALU.mult, ALU.add).then_inc(S("ve_y"), 1)
                if front:
                    mask(2)
                if front:
                    v.wait_ge(S("kv_psum"), s + 1)
                    if back:
                        v.wait_ge(S("state_ready"), s)
                    nc.vector.tensor_tensor(kvt.rearrange("p k b (h e) -> p (k b) h e", h=HB),
                                            bank[2][:].rearrange("p (k h e) -> p k h e", k=KB * BATCH, h=HB),
                                            headmask[:].rearrange("p (o h q) -> p o h q", o=1, q=1).to_broadcast([P, KB * BATCH, HB, DK]),
                                            ALU.mult).then_inc(S("kvt_ready"), 1)
                if front:
                    mask(3)

            def whole(x):
                return x.rearrange("p k b c -> p (k b c)")

            pair_step(0, True, False)
            v.wait_ge(S("rstd_x"), 2)
            with v.Fori(1, TB) as s:
                pair_step(s, True, True)
            pair_step(TB, False, True)
            v.wait_ge(S("rT_psum"), TB)
            def low_part(n, half, i):
                cols = slice(half * HALF, (half + 1) * HALF)
                src = wide[:, PROJECTION_BANKS[half][i], :]
                if i == 0:
                    v.wait_ge(S("khi_ready"), n * 2 + half + 1)
                    v.wait_ge(S("vT_ready"), n * 2 + half + 1)
                    nc.vector.tensor_tensor(klo[0:DH, cols], src[0:DH], khi[0:DH, cols].bitcast(F32), ALU.subtract).then_inc(S("klo_ready"), 1)
                else:
                    v.wait_ge(S("qhi_ready"), n * 4 + half * 2 + i)
                    for u in range(2):
                        h = 2 * (i - 1) + u
                        ins = nc.vector.scalar_tensor_tensor(out=qhl[DH:P, h, cols], in0=src[u * DH:(u + 1) * DH], scalar=DH ** -0.5,
                                                             in1=qhl[0:DH, h, cols].bitcast(F32), op0=ALU.mult, op1=ALU.subtract)
                    ins.then_inc(S("qlo_ready"), 1)

            for i in range(3):
                low_part(0, 0, i)
            with v.Fori(0, NKV) as g:
                for b in range(BATCH):
                    n = g * BATCH + b

                    def normalise(ct, h):
                        c = ct * G + h
                        w = (ct + 1) * P
                        v.wait_ge(S("exp_done"), n * (TB * G) + c + 1)
                        nc.vector.reciprocal(rinv[:, ct % 3, h:h + 1], rsum[:, ct % 3, h:h + 1]).then_inc(S("rinv_ready"), 1)
                        v.wait_ge(S("rinv_ready"), n * (TB * G) + c + 1)
                        nc.vector.tensor_scalar(probs[ct % 3][:, h, 0:w], probs[ct % 3][:, h, 0:w],
                                                rinv[:, ct % 3, h:h + 1], None, ALU.mult).then_inc(S("probs_ready"), 1)

                    last = None
                    for r, (score, turned, weighed, complete, project, add) in enumerate(rounds()):
                        if score:
                            ct, h = score
                            w = (ct + 1) * P
                            v.wait_ge(S("scores2"), n * (TB * G) + ct * G + h + 1)
                            nc.vector.tensor_reduce(nmax[:, ct % 3, h:h + 1],
                                                    wide[:, 2 * (h % 2):2 * (h % 2) + 2, :].rearrange("p a b -> p (a b)")[:, 0:w],
                                                    AX.X, ALU.max, negate=True).then_inc(S("nmax_ready"), 1)
                        for ct, m in turned:
                            j = pair(ct, m)
                            if evacuates(j) == "vector":
                                v.wait_ge(S("pT_psum"), n * PAIRS + j + 1)
                                nc.vector.tensor_copy(pT[j % 4], bank[1][:]).then_inc(S("pT_odd"), 1)
                        if last:
                            normalise(*last)
                        last = score
                        if r - 2 in SECOND_HALF:
                            low_part(n, 1, SECOND_HALF[r - 2])
                        if r - 1 in NEXT_FIRST_HALF:
                            low_part(n + 1, 0, NEXT_FIRST_HALF[r - 1])
                        if r == VALUES:
                            v.wait_ge(S("v2_psum"), n + 1)
                            nc.vector.tensor_copy(vt[:], bank[3][:].rearrange("p (t d) -> p t d", t=TB)).then_inc(S("v2_ready"), 1)
                        for ct in add:
                            v.wait_ge(S("proj2"), n * TB + ct + 1)
                            at = acc[:, b * TB + ct]
                            nc.vector.tensor_tensor(at, bank[3][:, 0:D], at, ALU.add).then_inc(S("acc_done"), 1)
            v.wait_ge(S("acc_done"), BATCH * NKV * TB)
            for t in range(NT // 4):
                v.wait_ge(S("hT_psum"), 2 * t + 2)
                nc.vector.tensor_copy(hT[:, 1, t * 4 * P:(t + 1) * 4 * P], turned_bank(t, 1)).then_inc(S("hT1_ready"), 1)
            v.wait_ge(S("hss_ready"), 1)
            nc.vector.tensor_scalar(hve[:], hss[:], 1.0 / D, EPS, ALU.mult, ALU.add).then_inc(S("ve_h"), 1)
            v.wait_ge(S("rstd_h"), 1)
            steps = [0]

            def step(ins):
                steps[0] += 1
                ins.then_inc(S("router_steps"), 1)
                v.wait_ge(S("router_steps"), steps[0])

            def over_experts(x):
                return x.rearrange("p (t o) -> p t o", o=1).to_broadcast([P, NT, E])

            v.wait_ge(S("logits_psum"), 1)
            logits = wide[:, 0, 0:NT * E].rearrange("p (t e) -> p t e", t=NT)
            step(nc.vector.tensor_tensor(glog[:], logits, over_experts(hrstd[:]), ALU.mult))
            step(nc.vector.tensor_reduce(gmax[:], glog[:], AX.X, ALU.max))
            nc.vector.tensor_tensor(glog[:], glog[:], over_experts(gmax[:]), ALU.subtract).then_inc(S("glog_ready"), 1)
            v.wait_ge(S("gexp_ready"), 1)
            step(nc.vector.tensor_reduce(gsum[:], glog[:], AX.X, ALU.add))
            step(nc.vector.reciprocal(gsum[:], gsum[:]))
            step(nc.vector.tensor_tensor(glog[:], glog[:], over_experts(gsum[:]), ALU.mult))
            for t in range(NT):
                ins = nc.vector.max(top[:, t], glog[:, t])
            step(ins)
            for t in range(NT):
                ins = nc.vector.max_index(topi[:, t], top[:, t], glog[:, t])
            step(ins)
            step(nc.vector.tensor_copy(topf[:], topi[:, :, 0:TOPK]))
            step(nc.vector.tensor_tensor(gsum[:], top[:, :, 0], top[:, :, 1], ALU.add))
            step(nc.vector.reciprocal(gmax[:], gsum[:]))
            step(nc.vector.tensor_tensor(topw[:], top[:, :, 0:TOPK], gmax[:].rearrange("p (t o) -> p t o", o=1).to_broadcast([P, NT, TOPK]), ALU.mult))
            for k in range(TOPK):
                ins = nc.vector.tensor_tensor(pick[:, k], experts[:].rearrange("p (e o) -> p e o", o=1).to_broadcast([P, E, NT]),
                                              topf[:, :, k].rearrange("p (o t) -> p o t", o=1).to_broadcast([P, E, NT]), ALU.is_equal)
            step(ins)
            step(nc.vector.tensor_tensor(picked[:], pick[:, 0], pick[:, 1], ALU.add))
            v.wait_ge(S("ranks_psum"), 1)
            flat = "p e t -> p (e t)"
            within = bank[0][:, 0:E * NT].rearrange("p (e t) -> p e t", e=E)
            totals = bank[1][:, 0:E * NT].rearrange("p (e t) -> p e t", e=E)
            step(nc.vector.tensor_tensor_scan(upto[:].rearrange(flat), restart[:].rearrange(flat), totals.rearrange(flat), 0.0, ALU.mult, ALU.add))
            step(nc.vector.tensor_tensor(full[:], upto[:, :, NT - 1:NT].to_broadcast([P, E, NT]),
                                         hundreds[:].rearrange("p (o t) -> p o t", o=1).to_broadcast([P, E, NT]), ALU.is_gt))
            step(nc.vector.tensor_reduce(nslots[:], full[:], AX.X, ALU.add))
            step(nc.vector.tensor_tensor_scan(endslot[:], ones[:, 0:E], nslots[:], 0.0, ALU.mult, ALU.add))
            step(nc.vector.tensor_tensor(passed[:], slotno[:].rearrange("p (s o) -> p s o", o=1).to_broadcast([1, NS, E]),
                                         endslot[0:1].rearrange("p (o e) -> p o e", o=1).to_broadcast([1, NS, E]), ALU.is_ge))
            step(nc.vector.tensor_reduce(slote[:], passed[:], AX.X, ALU.add))
            step(nc.vector.tensor_scalar(slotm[:], slote[:], float(E - 1), None, ALU.min))
            step(nc.vector.tensor_tensor(change[:, 1:NS], slotm[:, 1:NS], slotm[:, 0:NS - 1], ALU.not_equal))
            step(nc.vector.tensor_tensor(loads[:], change[:], starts[:], ALU.max))
            nc.vector.tensor_copy(freshi[:], loads[:])
            nc.vector.tensor_copy(slotei[:], slotm[:]).then_inc(S("slots_known"), 1)
            step(nc.vector.tensor_tensor(startrow[:], endslot[:], nslots[:], ALU.subtract))
            step(nc.vector.tensor_tensor(place[:], upto[:], totals, ALU.subtract))
            step(nc.vector.scalar_tensor_tensor(out=place[:], in0=startrow[:].rearrange("p (e o) -> p e o", o=1).to_broadcast([P, E, NT]), scalar=float(P),
                                                in1=place[:], op0=ALU.mult, op1=ALU.add))
            step(nc.vector.tensor_tensor(place[:], within, place[:], ALU.add))
            for k in range(TOPK):
                ins = nc.vector.tensor_tensor(prod[:, k], pick[:, k], place[:], ALU.mult)
            step(ins)
            for k in range(TOPK):
                ins = nc.vector.tensor_reduce(row[:, k], prod[:, k].rearrange("p e t -> p t e"), AX.X, ALU.add)
            step(ins)
            step(nc.vector.tensor_scalar(row[:], row[:], -1.0, None, ALU.add))
            nc.vector.tensor_copy(rowi[:], row[:]).then_inc(S("rows_known"), 1)

            with v.Fori(0, NS // UR) as it:
                for u in range(UR):
                    slot = it * UR + u
                    for half in range(2):
                        v.wait_ge(S("relu_ready"), slot * 2 + half + 1)
                        v.wait_ge(S("gate_psum"), slot * 2 + half + 1)
                        nc.vector.tensor_tensor(gated[:, half * 4:half * 4 + 4].rearrange("p f c -> p (f c)"), wide[:, 2 + half, :], relu[half],
                                                ALU.mult).then_inc(S("gated_ready"), 1)
            for quarter in range(4):
                tiles = range(quarter * (NT // 4), (quarter + 1) * (NT // 4))
                v.wait_ge(S(f"gathered{quarter}"), 16 * TOPK * (NT // 4))
                for k in range(TOPK):
                    for i in tiles:
                        ins = nc.vector.scalar_tensor_tensor(out=acc[:, i], in0=yg[:, i, k], scalar=topw[:, i, k:k + 1], in1=acc[:, i],
                                                             op0=ALU.mult, op1=ALU.add)
                    ins.then_inc(S("weighed"), 1)
                    v.wait_ge(S("weighed"), TOPK * quarter + k + 1)
                for i in tiles:
                    ins = nc.vector.bn_stats(stf[:, i], acc[:, i])
                ins.then_inc(S("ve_f_st"), 1)
                v.wait_ge(S("ve_f_st"), quarter + 1)
                for i in tiles:
                    ins = nc.vector.bn_aggr(hmean[:, i], stf[:, i])
                ins.then_inc(S("mean_f"), 1)
                v.wait_ge(S("std_f"), quarter + 1)
                nc.vector.reciprocal(hrstd[:, tiles[0]:tiles[-1] + 1], hve[:, tiles[0]:tiles[-1] + 1]).then_inc(S("rstd_f"), 1)
                v.wait_ge(S("rstd_f"), quarter + 1)
                for i in tiles:
                    nc.vector.tensor_scalar(acc[:, i], acc[:, i], hmean[:, i, 0:1], hrstd[:, i:i + 1], ALU.subtract, ALU.mult).then_inc(S("fn_ready"), 1)
                for i in tiles:
                    v.wait_ge(S("fn_ready"), i + 1)
                    nc.vector.tensor_tensor(x_all[:, i], x_all[:, i], acc[:, i], ALU.add).then_inc(S("out_ready"), 1)

        @block.tensor
        def _(pe):
            mm = nc.tensor.matmul
            pe.wait_ge(S("constants_ready"), NCONST)
            pe.wait_ge(S("small_loaded"), 16 * 9)
            mm(bank[3][:, 0:4 * DK + 5], rep[:].rearrange("p h e -> p (h e)"), small[:], start=True, stop=True).then_inc(S("small_psum"), 1)
            pe.wait_ge(S("wnat_loaded"), 64)
            pe.wait_ge(S("fdiag_ready"), 1)
            pe.wait_ge(S("smallr_ready"), 1)
            for w, to in ((2, bank[2]), (3, bank[3])):
                for k in range(KB):
                    for f in range(KB):
                        ins = nc.tensor.transpose(to[:, (k * KB + f) * P:(k * KB + f + 1) * P], wnat[:, w, f, k * P:(k + 1) * P], ident[:])
                ins.then_inc(S("wT_psum"), 1)
            for n in range(4):
                for k in range(KB):
                    for f in range(KB):
                        ins = mm(wide[:, n, (k * KB + f) * P:(k * KB + f + 1) * P], wnat[:, n // 2, f, k * P:(k + 1) * P],
                                 fdiagT[:, n].rearrange("p h e -> p (h e)"), start=True, stop=True)
                ins.then_inc(S("wfeat_psum"), 1)
            pe.wait_ge(S("wT_ready"), 2)
            pe.wait_ge(S("wfeat_ready"), 4)

            def pair_step(s, front, back):
                def turn(to, src, given):
                    for k in range(KB):
                        for b in range(BATCH):
                            ins = nc.tensor.transpose(to[:, (k * BATCH + b) * P:(k * BATCH + b + 1) * P], src(k, b), ident[:])
                    ins.then_inc(S(given), 1)

                def feature(to, n, given):
                    for f in range(KB):
                        for k in range(KB):
                            ins = mm(to[:, f * BATCH * P:(f + 1) * BATCH * P], wfeat[:, n, k, f * P:(f + 1) * P],
                                     xnT[:, k].rearrange("p b c -> p (b c)"), start=(k == 0), stop=(k == KB - 1))
                    ins.then_inc(S(given), 1)

                def score(half):
                    k, b = half // 2, half % 2
                    pe.wait_ge(S("qx0_ready" if k == 0 else "qx1_ready"), 2 * s + b + 1 if k == 0 else s + 1)
                    if back or half >= 2:
                        pe.wait_ge(S("sm_ready"), 4 * s + half - 1)
                    for j in range(2):
                        ins = mm(wide[:, 2 * b + j, :], kT[:, k, b], qx[:, k, b, j * 4:(j + 1) * 4].rearrange("p h c -> p (h c)"), start=True, stop=True)
                    ins.then_inc(S("scores1"), 1)

                def output(k):
                    for b in range(BATCH):
                        for m in range(3):
                            for j in range(4):
                                dst = bank[2][j * 32:(j + 1) * 32, (k * BATCH + b) * P:(k * BATCH + b + 1) * P]
                                if m == 0:
                                    mm(dst, state[:, k, b, j * 32:(j + 1) * 32], qT[:, k, b], start=True, stop=False)
                                else:
                                    ins = mm(dst, vpad[:, b, k, j, m - 1], sm[:, k, b, 2 * j + m - 1], start=False, stop=(m == 2))
                    return ins

                if back:
                    pe.wait_ge(S("sm_ready"), 4 * s - 2)
                    pe.wait_ge(S("v_ready"), s)
                    pe.wait_ge(S("kvt_ready"), s)
                    if front:
                        pe.wait_ge(S("state_ready"), s - 1)
                    else:
                        pe.wait_ge(S("state_ready"), TB - 1)
                    output(0)
                if front:
                    pe.wait_ge(S("xn_ready"), s + 1)
                    if back:
                        pe.wait_ge(S("v_ready"), s)
                    turn(bank[3], lambda k, b: xn[:, b, k * P:(k + 1) * P], "xnT_psum")
                if back:
                    pe.wait_ge(S("sm_ready"), 4 * s)
                    output(1).then_inc(S("o_psum"), 1)
                if front:
                    pe.wait_ge(S("xnT_ready"), s + 1)
                    if back:
                        pe.wait_ge(S("aon_ready"), s - 1)
                    feature(bank[0], 0, "q1_psum")
                if back:
                    pe.wait_ge(S("osq_ready"), s)
                    mm(bank[3][:], bd[:].rearrange("p h e -> p (h e)"), osq.rearrange("p k b c -> p (k b c)"), start=True, stop=True).then_inc(S("oms_psum"), 1)
                if front:
                    if back:
                        pe.wait_ge(S("rT_ready"), s - 1)
                    feature(bank[1], 1, "q2_psum")
                if front:
                    pe.wait_ge(S("q1_ready"), s + 1)
                    feature(bank[0], 2, "k1_psum")
                    pe.wait_ge(S("qT_ready"), s + 1)
                    feature(bank[1], 3, "k2_psum")
                if back:
                    pe.wait_ge(S("onT_ready"), s)
                    if front:
                        pe.wait_ge(S("k1_ready"), s + 1)
                    for b in range(BATCH):
                        for k in range(KB):
                            ins = mm(bank[0][:, b * D:(b + 1) * D], onT[:, k, b], woT[:, k], start=(k == 0), stop=(k == KB - 1))
                    ins.then_inc(S("ao_psum"), 1)
                if front:
                    if back:
                        pe.wait_ge(S("oms_ready"), s)
                    for b in range(BATCH):
                        for k in range(KB):
                            ins = mm(bank[3][:, b * D:(b + 1) * D], xnT[:, k, b], wvT[:, k], start=(k == 0), stop=(k == KB - 1))
                    ins.then_inc(S("v_psum"), 1)
                if front:
                    pe.wait_ge(S("kT_ready"), s + 1)
                    turn(bank[1], lambda k, b: kT[:, k, b], "ktok_psum")
                    score(0)
                    score(1)
                    score(2)
                    pe.wait_ge(S("ktok_ready"), s + 1)
                    pe.wait_ge(S("v_ready"), s + 1)
                    if back:
                        pe.wait_ge(S("onT_ready"), s)
                    for k in range(KB):
                        for b in range(BATCH):
                            ins = mm(bank[2][:, (k * BATCH + b) * P:(k * BATCH + b + 1) * P], ktok[:, k, b],
                                     vp[:, b, 4 * k:4 * (k + 1), 0:4:3], start=True, stop=True)
                    ins.then_inc(S("kv_psum"), 1)
                    score(3)
                if back:
                    pe.wait_ge(S("r_ready"), s)
                    if front:
                        pe.wait_ge(S("ktok_ready"), s + 1)
                    turn(bank[1], lambda k, b: rn[:, b, k * P:(k + 1) * P], "rT_psum")

            pair_step(0, True, False)
            with pe.Fori(1, TB) as s:
                pair_step(s, True, True)
            pair_step(TB, False, True)

            pe.wait_ge(S("rT_ready"), TB)

            def project_in(n, half, i, b):
                to = wide[:, PROJECTION_BANKS[half][i], :]
                if half:
                    pe.wait_ge(S("klo_ready" if i == 2 else "qlo_ready"), 2 * n + 2 if i == 2 else 4 * n + i + 1)
                for k in range(KB):
                    w = wkv_g[:, k] if i == 0 else wq_g[:, k, (i - 1) * P:i * P]
                    at = b * SEQ + half * HALF
                    ins = mm(to, w, rT_all[:, k, at:at + HALF], start=(k == 0), stop=(k == KB - 1))
                ins.then_inc(S("projected"), 1)

            for name in ("wq_loaded", "wk_loaded", "wv_loaded"):
                pe.wait_ge(S(name), 16)
            for i in range(3):
                project_in(0, 0, i, 0)
            with pe.Fori(0, NKV) as g:
                for b in range(BATCH):
                    n = g * BATCH + b

                    def score(ct, h):
                        c = ct * G + h
                        if c == 0:
                            pe.wait_ge(S("k_doubled"), n * 2 + 1)
                            pe.wait_ge(S("qlo_ready"), n * 4 + 1)
                        if c == 1:
                            pe.wait_ge(S("qlo_ready"), n * 4 + 2)
                        if c == TB // 2 * G:
                            pe.wait_ge(S("k_doubled"), n * 2 + 2)
                            pe.wait_ge(S("qlo_ready"), n * 4 + 4)
                        if c >= 2:
                            pe.wait_ge(S("exp_done"), n * (TB * G) + c - 1)
                        w = (ct + 1) * P
                        for lo in range(0, w, 512):
                            hi = min(w, lo + 512)
                            dst = wide[:, 2 * (h % 2) + lo // 512, 0:hi - lo]
                            q = qhl[:, h, ct * P:(ct + 1) * P]
                            mm(dst, q, khi[:, lo:hi], start=True, stop=False)
                            if hi == w:
                                mm(dst[:, w - P - lo:w - lo], identb[:], above[:], start=False, stop=False)
                            ins = mm(dst, q, klo[:, lo:hi], start=False, stop=True)
                        ins.then_inc(S("scores2"), 1)

                    def weigh(ct, m):
                        j = pair(ct, m)
                        pe.wait_ge(S("pT_odd" if j % 2 else "pT_even"), n * (PAIRS // 2) + j // 2)
                        if m == 0:
                            pe.wait_ge(S("probs_ready"), n * (TB * G) + (ct + 1) * G)
                        for h in range(G):
                            ins = nc.tensor.transpose(bank[j % 2][:, h * P:(h + 1) * P], probs[ct % 3][:, h, m * P:(m + 1) * P], ident[:])
                        ins.then_inc(S("pT_psum"), 1)

                    def values(ct, m):
                        j = pair(ct, m)
                        pe.wait_ge(S("pT_odd" if j % 2 else "pT_even"), n * (PAIRS // 2) + j // 2 + 1)
                        if ct == 0:
                            pe.wait_ge(S("v2_ready"), n + 1)
                        if m == 0:
                            pe.wait_ge(S("oT_ready"), n * TB + ct)
                        for u in range(2):
                            ins = mm(bank[2][u * DH:(u + 1) * DH, 0:2 * P], vt[:, m], pT[j % 4][:, u * 2 * P:(u + 1) * 2 * P],
                                     start=(m == 0), stop=(m == ct))
                        if m == ct:
                            ins.then_inc(S("o2_psum"), 1)

                    for r, (score_, turned, weighed, complete, project, add) in enumerate(rounds()):
                        if score_:
                            score(*score_)
                        if r in SECOND_HALF:
                            project_in(n, 1, SECOND_HALF[r], b)
                        if r in NEXT_FIRST_HALF:
                            if NEXT_FIRST_HALF[r] == 0:
                                pe.wait_ge(S("exp_done"), (n + 1) * (TB * G))
                                if b == BATCH - 1:
                                    for name in ("wq_loaded", "wk_loaded", "wv_loaded"):
                                        pe.wait_ge(S(name), 16 * g + 32)
                            project_in(n + 1, 0, NEXT_FIRST_HALF[r], (b + 1) % BATCH)
                        if r == VALUES:
                            wait_alone(pe, S("vT_ready"), n * 2 + 2)
                            wait_alone(pe, S("acc_done"), n * TB)
                            for t in range(TB):
                                ins = nc.tensor.transpose(bank[3][:, t * DH:(t + 1) * DH], vT[:, t * P:(t + 1) * P], ident[0:DH, 0:DH])
                            ins.then_inc(S("v2_psum"), 1)
                        after = dict(weighed)
                        for block_ in turned:
                            weigh(*block_)
                            if block_ in after:
                                values(*after[block_])
                        for turned_, block_ in weighed:
                            if turned_ is None:
                                values(*block_)
                        for ct in project:
                            pe.wait_ge(S("oT_ready"), n * TB + ct + 1)
                            pe.wait_ge(S("acc_done"), n * TB + ct)
                            if ct == 0:
                                pe.wait_ge(S("wo2_loaded"), 16 * 2 * NKV)
                                pe.wait_ge(S("v2_ready"), n + 1)
                            for j in range(2):
                                ins = mm(bank[3][:, 0:D], oT[:, j], wo2[:, bass.ds(g, 1), j].rearrange("p o d -> p (o d)"), start=(j == 0), stop=(j == 1))
                            ins.then_inc(S("proj2"), 1)

            pe.wait_ge(S("acc_done"), BATCH * NKV * TB)
            for t in range(NT // 4):
                for k in range(KB):
                    for q in range(4):
                        ins = nc.tensor.transpose(turned_bank(t, k)[:, q * P:(q + 1) * P], acc[:, 4 * t + q, k * P:(k + 1) * P], ident[:])
                    ins.then_inc(S("hT_psum"), 1)
            pe.wait_ge(S("gate_ready"), 1)
            for i in range(NT):
                pe.wait_ge(S("hT0_ready"), i // 4 + 1)
                pe.wait_ge(S("hT1_ready"), i // 4 + 1)
                for k in range(KB):
                    ins = mm(wide[:, 0, i * E:(i + 1) * E], hT[:, k, i * P:(i + 1) * P], gate[:, k], start=(k == 0), stop=(k == KB - 1))
            ins.then_inc(S("logits_psum"), 1)
            pe.wait_ge(S("router_steps"), ROUTED)
            mm(bank[0][:, 0:E * NT], tri[:], picked[:].rearrange("p e t -> p (e t)"), start=True, stop=True)
            mm(bank[1][:, 0:E * NT], ones[:], picked[:].rearrange("p e t -> p (e t)"), start=True, stop=True).then_inc(S("ranks_psum"), 1)

            def turn_slot(u, n, loads):
                pe.wait_ge(S("sT_ready"), n)
                pe.wait_ge(S(f"xs_loaded{u}"), loads)
                for k in range(KB):
                    ins = nc.tensor.transpose(bank[3][:, k * P:(k + 1) * P], xs_sb[u][:, k * P:(k + 1) * P], ident[:])
                ins.then_inc(S("sT_psum"), 1)

            turn_slot(0, 0, 16)
            with pe.Fori(0, NS // UR) as it:
                for u in range(UR):
                    slot = it * UR + u
                    pe.wait_ge(S("sT_ready"), slot + 1)
                    pe.wait_ge(S("gated_ready"), slot * 2)
                    for half in range(2):
                        for at, w, name in ((0, "w1", "up_psum"), (2, "w3", "gate_psum")):
                            if half == 0:
                                pe.wait_ge(S(f"{w}_loaded{u}"), 16 * it + 16)
                            w = w1_e[u] if w == "w1" else w3_e[u]
                            for f in range(4):
                                for k in range(KB):
                                    ins = mm(wide[:, at + half, f * P:(f + 1) * P], w[:, k, (half * 4 + f) * P:(half * 4 + f + 1) * P], sT[u][:, k],
                                             start=(k == 0), stop=(k == KB - 1))
                            ins.then_inc(S(name), 1)
                    turn_slot((u + 1) % UR, slot + 1, 16 * it + (16 if u < UR - 1 else 32))
                    pe.wait_ge(S(f"w2_loaded{u}"), 16 * it + 16)
                    pe.wait_ge(S(f"y_ready{u}"), it)
                    for f in range(FB):
                        if f % 4 == 0:
                            pe.wait_ge(S("gated_ready"), slot * 2 + f // 4 + 1)
                        ins = mm(bank[u][:, 0:D], gated[:, f], w2_e[u][:, f], start=(f == 0), stop=(f == FB - 1))
                    ins.then_inc(S(f"slot_done{u}"), 1)


_INS = ["L0_attn_x", "L0_attn_wq", "L0_attn_wk", "L0_attn_wv", "L0_attn_wo", "L0_attn_fq1_w", "L0_attn_fq1_b", "L0_attn_fq2_w",
        "L0_attn_fq2_b", "L0_attn_fk1_w", "L0_attn_fk1_b", "L0_attn_fk2_w", "L0_attn_fk2_b", "L0_attn_norm_w", "L0_ffn_ln1_w",
        "L0_ffn_wq", "L0_ffn_wk", "L0_ffn_wv", "L0_ffn_wo", "L0_ffn_ln2_w", "L0_ffn_gate_w", "L0_ffn_w1", "L0_ffn_w2", "L0_ffn_w3"]


def kernel(**inputs):
    import numpy as _np
    import concourse.bacc as _bacc
    from concourse.bass_utils import run_bass_kernel_spmd as _run

    nc = _bacc.Bacc("TRN2", target_bir_lowering=False, num_devices=1)
    arrays, aps = {}, {}
    for name in _INS:
        x = _np.ascontiguousarray(inputs[name])
        arrays[f"in_{name}"] = x
        aps[name] = nc.dram_tensor(f"in_{name}", x.shape, mybir.dt.from_np(x.dtype), kind="ExternalInput").ap()
    out = nc.dram_tensor("out_0", (BATCH, SEQ, D), F32, kind="ExternalOutput").ap()
    build(nc, aps, out)
    r = _run(nc, [arrays], core_ids=[0])
    return r.results[0]["out_0"]
```
